# Optimizing a Trainium2 kernel written in Bass

```python
import numpy as np
import jax
import jax.numpy as jnp

def _softmax(x, axis=-1):
    return jax.nn.softmax(x, axis=axis)

def _gelu(x):
    return jax.nn.gelu(x, approximate=True)

def _silu(x):
    return jax.nn.silu(x)

def _sigmoid(x):
    return jax.nn.sigmoid(x)

def _layernorm(x, axis=-1, eps=1e-05):
    m = jnp.mean(x, axis=axis, keepdims=True)
    v = jnp.var(x, axis=axis, keepdims=True)
    return (x - m) / jnp.sqrt(v + eps)

def _scatter_add(tgt, idx, src, axis=0):
    return tgt.at[idx].add(src)

def _segment_sum(src, seg, n):
    return jax.ops.segment_sum(src, seg, n)
kernel_name = 'mk_flamingo_gated_d1_seqx_r8_662c69'

def setup_inputs(seed: int=0):
    np.random.seed(seed)
    _w = jnp.asarray

    def _rec_inputs():
        import jax
        import jax.numpy as jnp
        _rk = jax.random.key(seed)
        x = 7.22e-05 + 1 * jax.random.normal(jax.random.fold_in(_rk, 1), (16, 128, 256), jnp.float32)
        _lenS = 128 - jax.random.randint(jax.random.fold_in(_rk, 7), (16,), 0, max(1, 128 // 4) + 1, jnp.int32)
        _lenS2 = 128 - jax.random.randint(jax.random.fold_in(_rk, 8), (16,), 0, max(1, 128 // 4) + 1, jnp.int32)
        _ctx_2048P = jax.random.normal(jax.random.fold_in(_rk, 11), (16, 16, 256), jnp.float32)
        _ctx_2048c = jax.random.dirichlet(jax.random.fold_in(_rk, 511), 0.3 * jnp.ones((16,), jnp.float32), (16, 128))
        _ctx_2048t = jnp.einsum('bsk,bkd->bsd', _ctx_2048c, _ctx_2048P)
        _ctx_2048t = _ctx_2048t * jax.lax.rsqrt(jnp.mean(jnp.square(_ctx_2048t)) + 1e-12) * 0.953939
        ctx_2048 = -0.000514642 + 1.00011 * (_ctx_2048t + 0.3 * jax.random.normal(jax.random.fold_in(_rk, 611), (16, 128, 256), jnp.float32))
        _g = jax.random.normal(jax.random.fold_in(_rk, 9001), (2, 1), jnp.float32)
        _g = jnp.sign(_g) * jnp.maximum(jnp.abs(_g), 1.0) + (_g == 0) * 1.0
        g_xattn = _g[0]
        g_ffn = _g[1]
        return (x, ctx_2048, g_xattn, g_ffn)
    x, ctx_2048, g_xattn, g_ffn = _rec_inputs()

    def _L0_xattn_setup():
        import jax, jax.numpy as jnp
        import numpy as np
        D_MODEL = 256
        NUM_HEADS = 16
        HEAD_DIM = D_MODEL // NUM_HEADS

        def _fq_sym(x, axis):
            s = jnp.max(jnp.abs(x), axis=axis, keepdims=True) / 127.0
            s = jnp.maximum(s, 1e-08)
            q = jnp.clip(jnp.round(x / s), -127.0, 127.0) * s
            return x + jax.lax.stop_gradient(q - x)

        def _fq_unsigned(x, axis):
            s = jnp.max(x, axis=axis, keepdims=True) / 255.0
            s = jnp.maximum(s, 1e-08)
            q = jnp.clip(jnp.round(x / s), 0.0, 255.0) * s
            return x + jax.lax.stop_gradient(q - x)
        key = jax.random.key(seed)
        ks = jax.random.split(key, 8)
        B, N, M, C = (2, 256, 64, D_MODEL)
        return {'x': jax.random.normal(ks[0], (B, N, C), jnp.float32), 'cond': jax.random.normal(ks[1], (B, M, C), jnp.float32), 'Wq': jax.random.normal(ks[2], (C, C), jnp.float32) * 0.02, 'bq': jnp.zeros((C,), jnp.float32), 'Wkv': jax.random.normal(ks[3], (C, 2 * C), jnp.float32) * 0.02, 'bkv': jnp.zeros((2 * C,), jnp.float32), 'Wp': jax.random.normal(ks[4], (C, C), jnp.float32) * 0.02, 'bp': jnp.zeros((C,), jnp.float32)}
    _L0_xattn_all = _L0_xattn_setup()
    _L0_xattn_in = {k: v for k, v in _L0_xattn_all.items() if k in ('Wq', 'bq', 'Wkv', 'bkv', 'Wp', 'bp')}
    del _L0_xattn_all

    def _L0_ffn_setup():
        import jax, jax.numpy as jnp
        import numpy as np
        B, S, D = (2, 256, 256)
        I = 128
        E = 32
        K = 4
        NS = 1
        ALPHA = 7.0

        def _clamped_swiglu(x, wg, wu, wd):
            g = jnp.clip(x @ wg.T, -ALPHA, ALPHA)
            u = jnp.clip(x @ wu.T, -ALPHA, ALPHA)
            return jax.nn.silu(g) * u @ wd.T
        key = jax.random.key(seed)
        ks = jax.random.split(key, 9)
        s = 0.02
        return {'hidden': jax.random.normal(ks[0], (B, S, D), jnp.float32), 'router_w': jax.random.normal(ks[1], (E, D), jnp.float32) * s, 'expert_bias': jax.random.normal(ks[2], (E,), jnp.float32) * s, 'gate_w': jax.random.normal(ks[3], (E, I, D), jnp.float32) * s, 'up_w': jax.random.normal(ks[4], (E, I, D), jnp.float32) * s, 'down_w': jax.random.normal(ks[5], (E, D, I), jnp.float32) * s, 'shared_gate_w': jax.random.normal(ks[6], (NS * I, D), jnp.float32) * s, 'shared_up_w': jax.random.normal(ks[7], (NS * I, D), jnp.float32) * s, 'shared_down_w': jax.random.normal(ks[8], (D, NS * I), jnp.float32) * s}
    _L0_ffn_all = _L0_ffn_setup()
    _L0_ffn_in = {k: v for k, v in _L0_ffn_all.items() if k in ('router_w', 'expert_bias', 'gate_w', 'up_w', 'down_w', 'shared_gate_w', 'shared_up_w', 'shared_down_w')}
    del _L0_ffn_all
    return {'x': x, 'ctx_2048': ctx_2048, 'g_xattn': g_xattn, 'g_ffn': g_ffn, 'L0_xattn_Wq': _L0_xattn_in['Wq'], 'L0_xattn_bq': _L0_xattn_in['bq'], 'L0_xattn_Wkv': _L0_xattn_in['Wkv'], 'L0_xattn_bkv': _L0_xattn_in['bkv'], 'L0_xattn_Wp': _L0_xattn_in['Wp'], 'L0_xattn_bp': _L0_xattn_in['bp'], 'L0_ffn_router_w': _L0_ffn_in['router_w'], 'L0_ffn_expert_bias': _L0_ffn_in['expert_bias'], 'L0_ffn_gate_w': _L0_ffn_in['gate_w'], 'L0_ffn_up_w': _L0_ffn_in['up_w'], 'L0_ffn_down_w': _L0_ffn_in['down_w'], 'L0_ffn_shared_gate_w': _L0_ffn_in['shared_gate_w'], 'L0_ffn_shared_up_w': _L0_ffn_in['shared_up_w'], 'L0_ffn_shared_down_w': _L0_ffn_in['shared_down_w']}

def reference(x, ctx_2048, g_xattn, g_ffn, L0_xattn_Wq, L0_xattn_bq, L0_xattn_Wkv, L0_xattn_bkv, L0_xattn_Wp, L0_xattn_bp, L0_ffn_router_w, L0_ffn_expert_bias, L0_ffn_gate_w, L0_ffn_up_w, L0_ffn_down_w, L0_ffn_shared_gate_w, L0_ffn_shared_up_w, L0_ffn_shared_down_w):
    import jax
    import jax.numpy as jnp

    def _L0_xattn_ref(x, cond, Wq, bq, Wkv, bkv, Wp, bp):
        import jax, jax.numpy as jnp
        import numpy as np
        D_MODEL = 256
        NUM_HEADS = 16
        HEAD_DIM = D_MODEL // NUM_HEADS

        def _fq_sym(x, axis):
            s = jnp.max(jnp.abs(x), axis=axis, keepdims=True) / 127.0
            s = jnp.maximum(s, 1e-08)
            q = jnp.clip(jnp.round(x / s), -127.0, 127.0) * s
            return x + jax.lax.stop_gradient(q - x)

        def _fq_unsigned(x, axis):
            s = jnp.max(x, axis=axis, keepdims=True) / 255.0
            s = jnp.maximum(s, 1e-08)
            q = jnp.clip(jnp.round(x / s), 0.0, 255.0) * s
            return x + jax.lax.stop_gradient(q - x)
        B, N, C = x.shape
        H, hd = (NUM_HEADS, HEAD_DIM)
        q = (x @ Wq + bq).reshape(1, B * N, H, hd)
        kv = (cond @ Wkv + bkv).reshape(1, -1, 2, H, hd)
        k, v = (kv[:, :, 0], kv[:, :, 1])
        scale = 1.0 / np.sqrt(hd).astype(np.float32)
        q = jnp.transpose(q * scale, (0, 2, 1, 3))
        k = jnp.transpose(k, (0, 2, 1, 3))
        v = jnp.transpose(v, (0, 2, 1, 3))
        q = _fq_sym(q, axis=-1)
        k = _fq_sym(k, axis=-1)
        v = _fq_sym(v, axis=2)
        attn = jnp.einsum('bhqd,bhkd->bhqk', q, k)
        attn = jax.nn.softmax(attn.astype(jnp.float32), axis=-1)
        attn = _fq_unsigned(attn, axis=-1)
        out = jnp.einsum('bhqk,bhkd->bhqd', attn, v)
        out = jnp.transpose(out, (0, 2, 1, 3)).reshape(B, N, C)
        return out @ Wp + bp

    def _L0_ffn_ref(hidden, router_w, expert_bias, gate_w, up_w, down_w, shared_gate_w, shared_up_w, shared_down_w):
        import jax, jax.numpy as jnp
        import numpy as np
        B, S, D = (2, 256, 256)
        I = 128
        E = 32
        K = 4
        NS = 1
        ALPHA = 7.0

        def _clamped_swiglu(x, wg, wu, wd):
            g = jnp.clip(x @ wg.T, -ALPHA, ALPHA)
            u = jnp.clip(x @ wu.T, -ALPHA, ALPHA)
            return jax.nn.silu(g) * u @ wd.T
        Bb, Ss, Dd = hidden.shape
        flat = hidden.reshape(-1, Dd)
        T = flat.shape[0]
        logits = flat @ router_w.T
        scores = jnp.sqrt(jax.nn.softplus(logits))
        _, idx = jax.lax.top_k(scores + expert_bias, K)
        topv = jnp.take_along_axis(scores, idx, axis=1)
        topv = topv / (topv.sum(axis=-1, keepdims=True) + 1e-20)
        probs = jnp.zeros((T, E), flat.dtype).at[jnp.arange(T)[:, None], idx].set(topv)

        def body(acc, xs):
            wg, wu, wd, p = xs
            return (acc + p[:, None] * _clamped_swiglu(flat, wg, wu, wd), None)
        out, _ = jax.lax.scan(body, jnp.zeros_like(flat), (gate_w, up_w, down_w, probs.T))
        out = out + _clamped_swiglu(flat, shared_gate_w, shared_up_w, shared_down_w)
        return out.reshape(Bb, Ss, Dd)
    x = x + jnp.tanh(g_xattn[0]) * _L0_xattn_ref(_layernorm(x, axis=-1), ctx_2048, L0_xattn_Wq, L0_xattn_bq, L0_xattn_Wkv, L0_xattn_bkv, L0_xattn_Wp, L0_xattn_bp)
    x = x + jnp.tanh(g_ffn[0]) * _L0_ffn_ref(_layernorm(x, axis=-1), L0_ffn_router_w, L0_ffn_expert_bias, L0_ffn_gate_w, L0_ffn_up_w, L0_ffn_down_w, L0_ffn_shared_gate_w, L0_ffn_shared_up_w, L0_ffn_shared_down_w)
    return x

_drawn_inputs = setup_inputs


def setup_inputs(seed=0):
    import zlib

    import numpy as np

    out = dict(_drawn_inputs(seed))
    spreads = {'L0_xattn_bq': (0.0, 0.8), 'L0_xattn_bkv': (0.0, 0.316), 'L0_xattn_bp': (0.0, 0.1)}
    factors = {'ctx_2048': 5.375,
     'L0_xattn_Wq': 8.0,
     'L0_xattn_Wkv': 5.663,
     'L0_ffn_router_w': 8.0,
     'L0_ffn_expert_bias': 8.0,
     'L0_ffn_gate_w': 8.0,
     'L0_ffn_up_w': 8.0,
     'L0_ffn_down_w': 8.0,
     'L0_ffn_shared_gate_w': 5.138,
     'L0_ffn_shared_up_w': 5.13,
     'L0_ffn_shared_down_w': 5.112}
    for name, (base, spread) in spreads.items():
        noise = np.random.default_rng([zlib.crc32(name.encode()), seed]).standard_normal(out[name].shape)
        drawn = base * np.exp(spread * noise) if base else spread * noise
        out[name] = jnp.asarray(drawn.astype(out[name].dtype))
    for name, factor in factors.items():
        out[name] = (out[name] * factor).astype(out[name].dtype)
    return out
```

```python
from contextlib import ExitStack

import numpy as np
import concourse.bass as bass
from concourse import mybir

ALU = mybir.AluOpType
ACT = mybir.ActivationFunctionType
AX = mybir.AxisListType
F32 = mybir.dt.float32
BF16 = mybir.dt.bfloat16
F16 = mybir.dt.float16
U8 = mybir.dt.uint8
U16 = mybir.dt.uint16

P = 128
ROUND = 1.5 * 2.0 ** 23
OFFSET = 1024.0


class Stage:

    def __init__(self, sem, step=1):
        self.sem, self.step, self.count = sem, step, 0

    def mark(self, instruction):
        instruction.then_inc(self.sem, self.step)
        self.count += self.step
        return self.sem, self.count


class Engine:

    def __init__(self, eng):
        self.eng, self.seen = eng, {}

    def need(self, *steps):
        for step in steps:
            if step is None:
                continue
            sem, value = step
            if self.seen.get(id(sem), 0) < value:
                self.seen[id(sem)] = value
                self.eng.wait_ge(sem, value)
        return self.eng


def build(nc, io):
    T, D = io["x"].shape
    H, HD = 16, D // 16
    E, S4 = io["router_wT"].shape[1], 4
    I = io["gateT"].shape[2]
    NT, C = T // P, D // P
    PAIRS = H // 2
    NE = E + 1
    LN255 = float(np.log(np.float64(255.0)))

    with ExitStack() as ctx:
        scopes = [ctx]

        def sb(name, shape, dt=F32):
            return scopes[-1].enter_context(nc.sbuf_tensor(name, shape, dt))

        def open_scope():
            scopes.append(ExitStack())

        def close_scope():
            scopes.pop().close()

        def stage(name, step=1):
            return Stage(ctx.enter_context(nc.semaphore(name)), step)

        pe, dve, act, pool, sp = (Engine(e) for e in (nc.tensor, nc.vector, nc.scalar, nc.gpsimd, nc.sync))

        x_sb = sb("x_sb", [P, NT, D])
        xn = sb("xn", [P, NT, D])
        xT = sb("xT", [P, C, T])
        cT = sb("cT", [P, C, T])
        wq = sb("wq", [P, C, D])
        wkv = sb("wkv", [P, C, 2 * D])
        wp = sb("wp", [P, C, D])
        rows = sb("rows", [1, 3 * D + 2])
        bv = sb("bv", [P, C])
        wr = sb("wr", [P, C, E])
        eb = sb("eb", [1, E])
        ones = sb("ones", [1, P])
        ident = sb("ident", [P, P])
        ident_b = sb("ident_b", [P, P], BF16)
        ident_h = sb("ident_h", [P, P], F16)
        gates = sb("gates", [P, 2])
        less_offset = sb("less_offset", [P, 1])
        S_ps = ctx.enter_context(nc.psum_tensor("S_ps", [P, 3, 2, 512], F32))
        T_ps = ctx.enter_context(nc.psum_tensor("T_ps", [P, 1, 512], F32))
        O_ps = ctx.enter_context(nc.psum_tensor("O_ps", [P, 2, D], F32))

        ld_x = stage("ld_x", 16)
        ld_w = stage("ld_w", 16)
        ld_c = stage("ld_c", 16)
        ld_l = stage("ld_l", 16)
        got_x = ld_x.mark(nc.sync.dma_start(x_sb[:], io["x"].rearrange("(n p) d -> p n d", p=P)))
        for src, dst in ((io["wq"], wq), (io["wkv"], wkv)):
            got_w = ld_w.mark(nc.sync.dma_start(dst[:], src.rearrange("(c p) d -> p c d", p=P)))
        got_w = ld_w.mark(nc.sync.dma_start(rows[:], io["rows"]))
        got_w = ld_w.mark(nc.sync.dma_start(bv[:], io["bv"]))
        got_c = ld_c.mark(nc.scalar.dma_start(cT[:], io["ctxT"].rearrange("(c p) t -> p c t", p=P)))
        got_l = ld_l.mark(nc.scalar.dma_start(wp[:], io["wp"].rearrange("(c p) d -> p c d", p=P)))
        got_l = ld_l.mark(nc.scalar.dma_start(wr[:], io["router_wT"].rearrange("(c p) e -> p c e", p=P)))
        got_l = ld_l.mark(nc.scalar.dma_start(eb[:], io["expert_bias"]))

        consts = stage("consts")
        made = consts.mark(nc.gpsimd.memset(ident[:], 0.0))
        pool.need(made)
        made = consts.mark(nc.gpsimd.affine_select(out=ident[:], in_=ident[:], compare_op=ALU.not_equal, fill=1.0,
                                                   base=0, pattern=[[-1, P]], channel_multiplier=1))
        pool.need(made)
        consts.mark(nc.gpsimd.tensor_copy(ident_b[:], ident[:]))
        consts.mark(nc.gpsimd.tensor_copy(ident_h[:], ident[:]))
        consts.mark(nc.gpsimd.memset(less_offset[:], -OFFSET))
        got_const = consts.mark(nc.gpsimd.memset(ones[:], 1.0))

        chain = stage("chain")

        def then(instruction):
            dve.need(chain.mark(instruction))

        root_s = stage("root_s")

        def inverse_root(out, var, tmp, y, n):
            then(nc.vector.tensor_scalar(tmp, var, 1e-5, None, ALU.add))
            act.need((chain.sem, chain.count))
            got = root_s.mark(nc.scalar.activation(y, tmp, ACT.Sqrt))
            dve.need(got)
            then(nc.vector.reciprocal(out, y))
            then(nc.vector.tensor_tensor(out, out, tmp, ALU.mult))
            then(nc.vector.tensor_tensor(out, out, y, ALU.add))
            then(nc.vector.tensor_scalar(out, out, 0.5, None, ALU.mult))
            then(nc.vector.reciprocal(out, out))

        stats = sb("stats", [P, NT, 6])
        mv = sb("mv", [P, NT, 2])
        rstd = sb("rstd", [P, NT])
        root_t = sb("root_t", [P, NT])
        root_y = sb("root_y", [P, NT])
        normed = stage("normed")

        def layer_norm():
            for n in range(NT):
                ins = nc.vector.bn_stats(stats[:, n, :], x_sb[:, n, :])
            then(ins)
            for n in range(NT):
                ins = nc.vector.bn_aggr(mv[:, n, :], stats[:, n, :])
            then(ins)
            inverse_root(rstd[:], mv[:, :, 1], root_t[:], root_y[:], NT)
            steps = []
            for n in range(NT):
                steps.append(normed.mark(nc.vector.tensor_scalar(xn[:, n, :], x_sb[:, n, :], mv[:, n, 0:1],
                                                                 rstd[:, n:n + 1], ALU.subtract, ALU.mult)))
            return steps

        turned = stage("turned")
        turned_out = stage("turned_out")
        free = {}

        def bank(k):
            return S_ps[:, k // 2, k % 2, :]

        def turn(src, dst, ready):
            out = []
            for g in range(NT // 2):
                k = g % 2
                pe.need(got_const, ready[2 * g], ready[2 * g + 1], free.get(k))
                for c in range(C):
                    for n in range(2):
                        ins = nc.tensor.transpose(bank(k)[:, (2 * c + n) * P:(2 * c + n + 1) * P],
                                                  src[:, 2 * g + n, c * P:(c + 1) * P], ident[:])
                got = turned.mark(ins)
                act.need(got)
                step = turned_out.mark(nc.scalar.copy(dst[:, :, 2 * g * P:(2 * g + 2) * P],
                                                      bank(k).rearrange("p (c t) -> p c t", c=C)))
                free[k] = step
                out.append(step)
            return out

        dve.need(got_x)
        steps = layer_norm()
        xT_steps = turn(xn, xT, steps)

        open_scope()
        qT = sb("qT", [P, PAIRS, T], BF16)
        kT = sb("kT", [P, PAIRS, T], BF16)
        v_int = sb("v_int", [P, NT, D], BF16)
        sq = sb("sq", [P, NT, H])
        neg_sq = sb("neg_sq", [P, NT, H])
        open_scope()
        vT = sb("vT", [P, C, T])
        proj = stage("proj")
        q4 = sb("q4", [P, 2, 2, H, 4, HD], BF16)
        quant = sb("quant", [P, 2, H, HD])
        kfull = sb("kfull", [P, 2, H, HD])
        rest1 = sb("rest1", [P, 2, H, HD])
        amax = sb("amax", [P, 2, H])
        rec = sb("rec", [P, 2, H])
        sk = sb("sk", [P, 2, H])
        then(nc.vector.memset(q4[:], 0.0))
        ready4 = stage("ready4")
        turn4 = stage("turn4")
        out4 = stage("out4")
        buf4_free = [None, None]

        def heads(row, w, w0, src, src_steps, scale, dst, keep_scale, split, count):
            for g in range(NT // 2):
                k = 2 + g % 2
                b = g % 2
                pe.need(src_steps[g], got_w, got_const, free.get(k))
                for n in range(2):
                    o = bank(k)[:, n * D:(n + 1) * D]
                    for c in range(C):
                        nc.tensor.matmul(o, src[:, c, (2 * g + n) * P:(2 * g + n + 1) * P], w[:, c, w0:w0 + D],
                                         start=(c == 0), stop=False)
                    ins = nc.tensor.matmul(o, ones[:], rows[:, row * D:(row + 1) * D], start=False, stop=True)
                dve.need(proj.mark(ins))
                ps = bank(k).rearrange("p (n h d) -> p n h d", n=2, h=H)
                then(nc.vector.tensor_reduce(amax[:], ps, AX.X, ALU.max, apply_absolute_value=True))
                s = keep_scale[:, 2 * g:2 * g + 2, :] if keep_scale is not None else sk[:]
                then(nc.vector.tensor_scalar(s, amax[:], scale / 127.0, 1e-8, ALU.mult, ALU.max))
                then(nc.vector.reciprocal(rec[:], s))
                if scale != 1.0:
                    then(nc.vector.tensor_scalar(rec[:], rec[:], scale, None, ALU.mult))
                rb = rec[:].unsqueeze(3).broadcast_to([P, 2, H, HD])
                ins = nc.vector.tensor_tensor(quant[:], ps, rb, ALU.mult)
                then(ins)
                free[k] = (chain.sem, chain.count)
                then(nc.vector.tensor_scalar(quant[:], quant[:], 127.0, -127.0, ALU.min, ALU.max))
                dve.need(buf4_free[b])
                if not split:
                    for n in range(2):
                        ins = nc.vector.tensor_scalar(q4[:, b, n, :, 0:3, :],
                                                      quant[:, n].unsqueeze(2).broadcast_to([P, H, 3, HD]),
                                                      ROUND, ROUND, ALU.add, ALU.subtract)
                else:
                    then(nc.vector.tensor_scalar(quant[:], quant[:], ROUND, ROUND, ALU.add, ALU.subtract))
                    sb_ = sk[:].unsqueeze(3).broadcast_to([P, 2, H, HD])
                    then(nc.vector.tensor_tensor(kfull[:], quant[:], sb_, ALU.mult))
                    hi, mid, lo = (q4[:, b, :, :, j, :] for j in range(3))
                    then(nc.vector.tensor_copy(hi, kfull[:]))
                    then(nc.vector.tensor_tensor(rest1[:], kfull[:], hi, ALU.subtract))
                    then(nc.vector.tensor_copy(mid, rest1[:]))
                    ins = nc.vector.tensor_tensor(lo, rest1[:], mid, ALU.subtract)
                step = ready4.mark(ins)
                for n in range(2):
                    k2 = 4 + n
                    pe.need(step, free.get(k2))
                    tb = bank(k2).bitcast(BF16)
                    for pair in range(PAIRS):
                        ins = nc.tensor.transpose(tb[:, pair * P:(pair + 1) * P],
                                                  q4[:, b, n, 2 * pair:2 * pair + 2, :, :].rearrange("p h s d -> p (h s d)"),
                                                  ident_b[:])
                    act.need(turn4.mark(ins))
                    t0 = (2 * g + n) * P
                    free[k2] = out4.mark(nc.scalar.copy(dst[:, :, t0:t0 + P],
                                                        tb.rearrange("p (c t) -> p c t", c=PAIRS)))
                buf4_free[b] = (turn4.sem, turn4.count)
            return (out4.sem, out4.count)

        k_ready = heads(1, wkv, 0, cT, [got_c] * 8, 1.0, kT, None, True, 0)
        q_ready = heads(0, wq, 0, xT, xT_steps, 0.25, qT, sq, False, 1)
        then(nc.vector.tensor_scalar(neg_sq[:], sq[:], -1.0, None, ALU.mult))

        vproj = stage("vproj")
        vout = stage("vout")
        for c in range(C):
            for t in range(T // 512):
                k = t % 2
                pe.need(free.get(k))
                for d in range(C):
                    ins = nc.tensor.matmul(bank(k), wkv[:, d, D + c * P:D + (c + 1) * P],
                                           cT[:, d, t * 512:(t + 1) * 512], start=(d == 0), stop=(d == C - 1))
                act.need(vproj.mark(ins))
                free[k] = vout.mark(nc.scalar.activation(vT[:, c, t * 512:(t + 1) * 512], bank(k), ACT.Identity,
                                                         bias=bv[:, c:c + 1]))
        dve.need((vout.sem, vout.count))
        vmax = sb("vmax", [P, C])
        sv = sb("sv", [P, C])
        rv = sb("rv", [P, C])
        vTi = sb("vTi", [P, C, T], BF16)
        then(nc.vector.tensor_reduce(vmax[:], vT[:], AX.X, ALU.max, apply_absolute_value=True))
        then(nc.vector.tensor_scalar(sv[:], vmax[:], 1.0 / 127.0, 1e-8, ALU.mult, ALU.max))
        then(nc.vector.reciprocal(rv[:], sv[:]))
        for c in range(C):
            ins = nc.vector.tensor_scalar(vT[:, c, :], vT[:, c, :], rv[:, c:c + 1], 127.0, ALU.mult, ALU.min)
        then(ins)
        then(nc.vector.tensor_scalar(vT[:], vT[:], -127.0, ROUND, ALU.max, ALU.add))
        ins = nc.vector.tensor_scalar(vTi[:], vT[:], ROUND, None, ALU.subtract)
        v_round = ready4.mark(ins)
        dve.need(got_l)
        for c in range(C):
            ins = nc.vector.tensor_scalar(wp[:, c, :], wp[:, c, :], sv[:, c:c + 1], None, ALU.mult)
        then(ins)
        wp_scaled = (chain.sem, chain.count)
        for g in range(NT // 4):
            k = 2 + g % 2
            pe.need(v_round, free.get(k))
            tb = bank(k).bitcast(BF16)
            for n in range(4):
                for c in range(C):
                    ins = nc.tensor.transpose(tb[:, (2 * n + c) * P:(2 * n + c + 1) * P],
                                              vTi[:, c, (4 * g + n) * P:(4 * g + n + 1) * P], ident_b[:])
            act.need(turn4.mark(ins))
            free[k] = out4.mark(nc.scalar.copy(v_int[:, 4 * g:4 * g + 4, :], tb.rearrange("p (n d) -> p n d", n=4)))
        v_ready = (out4.sem, out4.count)

        close_scope()
        NB_E = 2
        words = sb("words", [P, NB_E, T], U16)
        pT = sb("pT", [P, 2, 2, T // 2], BF16)
        hmax = sb("hmax", [P, 4, 2])
        nbias = sb("nbias", [P, 4, 1])
        nb_t = sb("nb_t", [P, 4, 1])
        psums = sb("psums", [P, NT, H, 2])
        norm = sb("norm", [P, NT, H])
        pool.need(q_ready, k_ready, v_ready, wp_scaled)
        filled = consts.mark(nc.gpsimd.memset(words[:], 0x6400))
        heads_out = xn

        s_mm, s_max, s_bias, s_exp = stage("s_mm"), stage("s_max"), stage("s_bias"), stage("s_exp")
        s_turn, s_evac, s_pv, s_norm = stage("s_turn"), stage("s_evac"), stage("s_pv"), stage("s_norm")
        U = NT * H
        score, expd, turnd, evac, pvd, biasd = {}, {}, {}, {}, {}, {}
        normd = {}
        bytes_of = words[:].bitcast(U8).rearrange("p b (t two) -> p b t two", two=2)
        word_f16 = words[:].bitcast(F16)
        t_bank = T_ps[:, 0, :].bitcast(F16)

        def do_scores(u, half):
            t, h = divmod(u, H)
            j = 2 * u + half
            pe.need(k_ready, q_ready, expd.get(j - 3), free.get(2 * (j % 3)), free.get(2 * (j % 3) + 1))
            r = 64 * (h % 2)
            for m in range(2):
                k0 = (2 * half + m) * 512
                ins = nc.tensor.matmul(S_ps[:, j % 3, m, :], qT[r:r + 64, h // 2, t * P:(t + 1) * P],
                                       kT[r:r + 64, h // 2, k0:k0 + 512], start=True, stop=True)
            score[j] = s_mm.mark(ins)

        def do_max(u, half):
            j = 2 * u + half
            dve.need(score[j], biasd.get(u - 4))
            s_max.mark(nc.vector.tensor_reduce(hmax[:, u % 4, half:half + 1], S_ps[:, j % 3, :, :], AX.XY, ALU.max))

        def do_bias(u):
            t, h = divmod(u, H)
            dve.need((s_max.sem, s_max.count), expd.get(2 * (u - 4) + 1))
            then(nc.vector.scalar_tensor_tensor(out=nb_t[:, u % 4, :], in0=hmax[:, u % 4, 0:1],
                                                scalar=hmax[:, u % 4, 1:2], in1=neg_sq[:, t, h:h + 1],
                                                op0=ALU.max, op1=ALU.mult))
            biasd[u] = s_bias.mark(nc.vector.tensor_scalar(nbias[:, u % 4, :], nb_t[:, u % 4, :], LN255, None, ALU.add))

        def do_exp(u, half):
            t, h = divmod(u, H)
            j = 2 * u + half
            act.need(biasd[u], filled, turnd.get((u - NB_E, half)))
            expd[j] = s_exp.mark(nc.scalar.activation(
                bytes_of[:, u % NB_E, half * (T // 2):(half + 1) * (T // 2), 0:1],
                S_ps[:, j % 3, :, :].rearrange("p m (n o) -> p (m n) o", o=1), ACT.Exp,
                bias=nbias[:, u % 4, :], scale=sq[:, t, h:h + 1], accum_out=psums[:, t, h, half:half + 1]))

        def do_turn(u, half):
            pe.need(expd[2 * u + half], evac.get((u, 0)) if half else evac.get((u - 1, 1)))
            for m in range(NT // 2):
                k0 = (half * (NT // 2) + m) * P
                ins = nc.tensor.transpose(t_bank[:, m * P:(m + 1) * P], word_f16[:, u % NB_E, k0:k0 + P], ident_h[:])
            turnd[u, half] = s_turn.mark(ins)

        def do_evac(u, half):
            e = act if half == 0 else dve
            e.need(turnd[u, half], pvd.get((u - 2, half)))
            o = pT[:, u % 2, half, :]
            if half == 0:
                ins = nc.scalar.activation(o, t_bank, ACT.Identity, bias=less_offset[:])
            else:
                ins = nc.vector.tensor_scalar(o, t_bank, OFFSET, None, ALU.subtract)
            evac[u, half] = (s_evac if half else s_evac0).mark(ins)

        s_evac0 = stage("s_evac0")

        def do_pv(u, half):
            t, h = divmod(u, H)
            pe.need(evac[u, half], v_ready, normd.get(t - 1))
            for m in range(NT // 2):
                kt = half * (NT // 2) + m
                ins = nc.tensor.matmul(O_ps[:, t % 2, h * HD:(h + 1) * HD], pT[:, u % 2, half, m * P:(m + 1) * P],
                                       v_int[:, kt, h * HD:(h + 1) * HD], start=(kt == 0), stop=(kt == NT - 1))
            pvd[u, half] = s_pv.mark(ins)

        def do_norm(t):
            dve.need(pvd[t * H + H - 1, 1], expd[2 * (t * H + H - 1) + 1])
            n = norm[:, t, :]
            then(nc.vector.tensor_tensor(n, psums[:, t, :, 0], psums[:, t, :, 1], ALU.add))
            then(nc.vector.reciprocal(n, n))
            then(nc.vector.tensor_scalar(n, n, 1e-8, None, ALU.max))
            normd[t] = s_norm.mark(nc.vector.tensor_tensor(
                heads_out[:, t, :].rearrange("p (h d) -> p h d", h=H), O_ps[:, t % 2, :].rearrange("p (h d) -> p h d", h=H),
                n.unsqueeze(2).broadcast_to([P, H, HD]), ALU.mult))

        for i in range(U + 2):
            a, b = i - 1, i - 2
            if i < U:
                do_scores(i, 0)
            if 0 <= a < U:
                do_exp(a, 0)
            if i < U:
                do_max(i, 0)
            if b >= 0:
                do_turn(b, 1)
                do_evac(b, 1)
                do_pv(b, 0)
            if i < U:
                do_scores(i, 1)
                do_max(i, 1)
                do_bias(i)
            if 0 <= a < U:
                do_turn(a, 0)
                do_exp(a, 1)
                do_evac(a, 0)
            if b >= 0:
                do_pv(b, 1)
                if b % H == H - 1:
                    do_norm(b // H)

        close_scope()
        open_scope()
        for k in range(6):
            free[k] = expd[2 * U - 1]
        hT = cT
        hT_steps = turn(heads_out, hT, [normd[t] for t in range(NT)])
        s_gate = stage("s_gate")
        pe.need(expd[2 * U - 1], evac[U - 1, 1])
        ins = nc.tensor.matmul(T_ps[:, 0, 0:2], ones[:], rows[:, 3 * D:3 * D + 2], start=True, stop=True)
        act.need(s_gate.mark(ins))
        gate_step = s_gate.mark(nc.scalar.activation(gates[:], T_ps[:, 0, 0:2], ACT.Tanh))
        dve.need(gate_step)
        pe.need(wp_scaled)
        s_res = stage("s_res")
        for g in range(NT // 2):
            k = 2 + g % 2
            pe.need(hT_steps[g], free.get(k))
            for n in range(2):
                o = bank(k)[:, n * D:(n + 1) * D]
                for c in range(C):
                    nc.tensor.matmul(o, hT[:, c, (2 * g + n) * P:(2 * g + n + 1) * P], wp[:, c, :],
                                     start=(c == 0), stop=False)
                ins = nc.tensor.matmul(o, ones[:], rows[:, 2 * D:3 * D], start=False, stop=True)
            dve.need(proj.mark(ins))
            xo = x_sb[:, 2 * g:2 * g + 2, :].rearrange("p n d -> p (n d)")
            free[k] = s_res.mark(nc.vector.scalar_tensor_tensor(out=xo, in0=bank(k), scalar=gates[:, 0:1], in1=xo,
                                                                op0=ALU.mult, op1=ALU.add))
        dve.need((s_res.sem, s_res.count), (turned.sem, turned.count))
        steps = layer_norm()
        x2_steps = turn(xn, xT, steps)

        lg = sb("lg", [P, NT, E])
        sc = sb("sc", [P, NT, E])
        t1 = sb("t1", [P, NT, E])
        t2 = sb("t2", [P, NT, E])
        SENT = -3.0e38
        choose = sb("choose", [P, NT, E + 8])
        chosen = sb("chosen", [P, NT, E + 8])
        top = sb("top", [P, NT, 8])
        prob = sb("prob", [P, NT, NE])
        psum1 = sb("psum1", [P, NT])
        bank_lg = bank(4)
        s_lg = stage("s_lg")
        pe.need(got_l, free.get(4))
        for n in range(NT):
            pe.need(x2_steps[n // 2])
            for c in range(C):
                ins = nc.tensor.matmul(bank_lg[:, n * E:(n + 1) * E], xT[:, c, n * P:(n + 1) * P], wr[:, c, :],
                                       start=(c == 0), stop=(c == C - 1))
        lg_done = s_lg.mark(ins)
        pe.need(free.get(5))
        ins = nc.tensor.matmul(bank(5)[:, 0:E], ones[:], eb[:], start=True, stop=True)
        eb_done = s_lg.mark(ins)
        dve.need(eb_done)
        ps_lg = bank_lg.rearrange("p (n e) -> p n e", n=NT)
        then(nc.vector.tensor_copy(lg[:], ps_lg))
        then(nc.vector.tensor_scalar(t1[:], lg[:], -1.0, None, ALU.mult))
        then(nc.vector.tensor_tensor(t1[:], lg[:], t1[:], ALU.min))
        act.need((chain.sem, chain.count))
        s_rt = stage("s_rt")
        act.need(s_rt.mark(nc.scalar.activation(t2[:], t1[:], ACT.Exp)))
        got = s_rt.mark(nc.scalar.activation(t1[:], t2[:], ACT.Ln, bias=1.0))
        dve.need(got)
        then(nc.vector.scalar_tensor_tensor(out=t1[:], in0=lg[:], scalar=0.0, in1=t1[:], op0=ALU.max, op1=ALU.add))
        act.need((chain.sem, chain.count))
        got = s_rt.mark(nc.scalar.activation(t2[:], t1[:], ACT.Sqrt))
        dve.need(got)
        then(nc.vector.tensor_scalar(t2[:], t2[:], 1e-18, None, ALU.max))
        then(nc.vector.reciprocal(sc[:], t2[:]))
        then(nc.vector.tensor_tensor(sc[:], sc[:], t1[:], ALU.mult))
        then(nc.vector.tensor_tensor(sc[:], sc[:], t2[:], ALU.add))
        then(nc.vector.tensor_scalar(sc[:], sc[:], 0.5, None, ALU.mult))
        then(nc.vector.memset(choose[:], SENT))
        then(nc.vector.tensor_tensor(choose[:, :, 0:E], sc[:], bank(5)[:, 0:E].unsqueeze(1).broadcast_to([P, NT, E]),
                                     ALU.add))
        for n in range(NT):
            ins = nc.vector.max(top[:, n, :], choose[:, n, :])
        then(ins)
        then(nc.vector.memset(top[:, :, S4:8], SENT))
        for n in range(NT):
            ins = nc.vector.match_replace(chosen[:, n, :], top[:, n, :], choose[:, n, :], 2.0 * -1.5e38)
        then(ins)
        then(nc.vector.tensor_tensor(prob[:, :, 0:E], chosen[:, :, 0:E], choose[:, :, 0:E], ALU.not_equal))
        then(nc.vector.tensor_tensor(prob[:, :, 0:E], prob[:, :, 0:E], sc[:], ALU.mult))
        then(nc.vector.tensor_reduce(psum1[:], prob[:, :, 0:E], AX.X, ALU.add))
        then(nc.vector.tensor_scalar(psum1[:], psum1[:], 1e-20, None, ALU.add))
        then(nc.vector.reciprocal(psum1[:], psum1[:]))
        then(nc.vector.tensor_scalar(psum1[:], psum1[:], 0.5, None, ALU.mult))
        then(nc.vector.tensor_tensor(prob[:, :, 0:E], prob[:, :, 0:E],
                                     psum1[:].unsqueeze(2).broadcast_to([P, NT, E]), ALU.mult))
        then(nc.vector.memset(prob[:, :, E:NE], 0.5))
        probs_step = (chain.sem, chain.count)
        probT = sb("probT", [NE, T])
        s_pt = stage("s_pt")
        for g in range(4):
            k = g % 2
            pe.need(probs_step, free.get(k))
            for n in range(4):
                ins = nc.tensor.transpose(bank(k)[0:NE, n * P:(n + 1) * P], prob[:, 4 * g + n, :], ident[:])
            act.need(turned.mark(ins))
            free[k] = s_pt.mark(nc.scalar.copy(probT[:, 512 * g:512 * (g + 1)], bank(k)[0:NE, :]))
        sp.need((s_pt.sem, s_pt.count))
        st_p = stage("st_p", 16)
        probs_stored = st_p.mark(nc.sync.dma_start(io["prob_scratch"], probT[:]))

        TB = 1024
        NSUB = TB // 512
        NTB = TB // P
        WB = 3
        HB = 2
        wg_sb = sb("wg_sb", [P, WB, C, I])
        wu_sb = sb("wu_sb", [P, WB, C, I])
        wd_sb = sb("wd_sb", [P, WB, D])
        pb_sb = sb("pb_sb", [P, WB, TB])
        gc = sb("gc", [P, 2, 512])
        uc = sb("uc", [P, 2, 512])
        th = sb("th", [P, 2, 512])
        gp = sb("gp", [P, 2, 512])
        hid = sb("hid", [P, HB, TB])
        ld_e = [stage(f"ld_e{n}", 16) for n in range(WB)]
        s_gu, s_gc, s_uc, s_th, s_gp, s_st, s_hid, s_dn = (
            stage(n) for n in ("s_gu", "s_gc", "s_uc", "s_th", "s_gp", "s_st", "s_hid", "s_dn"))
        def out_tile(n):
            if n < 4:
                return bank(4 + n // 2)[:, (n % 2) * D:(n % 2 + 1) * D]
            if n < 6:
                return T_ps[:, 0, (n % 2) * D:(n % 2 + 1) * D]
            return O_ps[:, n % 2, :]
        result = [sb(f"result{n}", [P, D]) for n in range(NTB)]
        st_o = stage("st_o", 16)
        s_fin = stage("s_fin")
        sp.need(probs_stored)
        act.need(probs_stored)
        gu_ready, gc_d, uc_d, gp_d, hid_d, dn_d, th_d, st_d = {}, {}, {}, {}, {}, {}, {}, {}
        fin = []
        items = [(b, e) for b in range(T // TB) for e in range(NE)]

        def load(i):
            b, e = items[i]
            w = i % WB
            sp.need(dn_d.get(i - WB), gp_d.get((i - WB, NSUB - 1)))
            ld_e[w].mark(nc.sync.dma_start(wg_sb[:, w], io["gateT"][e].rearrange("(c p) i -> p c i", p=P)))
            ld_e[w].mark(nc.sync.dma_start(wu_sb[:, w], io["upT"][e].rearrange("(c p) i -> p c i", p=P)))
            ld_e[w].mark(nc.sync.dma_start(wd_sb[:, w], io["downT"][e]))
            return ld_e[w].mark(nc.sync.dma_start(pb_sb[:, w], io["prob_scratch"][e:e + 1, b * TB:(b + 1) * TB]
                                                  .broadcast_to([P, TB])))

        loaded = {i: load(i) for i in range(WB)}

        def gate_up(i, s):
            b, e = items[i]
            j = NSUB * i + s
            t0 = b * TB + s * 512
            pe.need(loaded[i], gc_d.get(j - 2), uc_d.get(j - 2), free.get(j % 2), free.get(2 + j % 2))
            for w, o in ((wg_sb, bank(j % 2)), (wu_sb, bank(2 + j % 2))):
                for c in range(C):
                    ins = nc.tensor.matmul(o, w[:, i % WB, c, :], xT[:, c, t0:t0 + 512], start=(c == 0), stop=(c == C - 1))
            gu_ready[j] = s_gu.mark(ins)

        def hidden(i, s):
            j = NSUB * i + s
            q = j % 2
            dve.need(gu_ready[j], gp_d.get((i - 1, s)) if NSUB == 2 else None, th_d.get(j - 2))
            gc_d[j] = s_gc.mark(nc.vector.tensor_scalar(gc[:, q, :], bank(q), 7.0, -7.0, ALU.min, ALU.max))
            uc_d[j] = s_uc.mark(nc.vector.tensor_scalar(uc[:, q, :], bank(2 + q), 7.0, -7.0, ALU.min, ALU.max))
            act.need(gc_d[j], st_d.get(j - 2))
            th_d[j] = s_th.mark(nc.scalar.activation(th[:, q, :], gc[:, q, :], ACT.Tanh, scale=0.5))
            pool.need(loaded[i], gc_d[j], st_d.get(j - 2))
            gp_d[i, s] = s_gp.mark(nc.gpsimd.tensor_tensor(gp[:, q, :], gc[:, q, :], pb_sb[:, i % WB, s * 512:(s + 1) * 512],
                                                           ALU.mult))
            dve.need(th_d[j], gp_d[i, s])
            st_d[j] = s_st.mark(nc.vector.scalar_tensor_tensor(out=gp[:, q, :], in0=th[:, q, :], scalar=1.0,
                                                               in1=gp[:, q, :], op0=ALU.add, op1=ALU.mult))
            dve.need(st_d[j], uc_d[j], dn_d.get(i - HB))
            hid_d[i, s] = s_hid.mark(nc.vector.tensor_tensor(hid[:, i % HB, s * 512:(s + 1) * 512], gp[:, q, :],
                                                             uc[:, q, :], ALU.mult))

        def down(i):
            b, e = items[i]
            if e == 0 and b > 0:
                pe.need(fin[-1])
            if i == 0:
                pe.need(*(free.get(k) for k in (4, 5)), gate_step, eb_done, probs_step, lg_done)
            for n in range(NTB):
                pe.need(hid_d[i, n * P // 512])
                ins = nc.tensor.matmul(out_tile(n), hid[:, i % HB, n * P:(n + 1) * P], wd_sb[:, i % WB, :],
                                       start=(e == 0 and n % 2 == 0), stop=(e == NE - 1), skip_group_check=True)
            dn_d[i] = s_dn.mark(ins)

        def finish(b):
            for n in range(NTB):
                r = result[n]
                t = b * NTB + n
                dve.need(dn_d[b * NE + NE - 1], (st_o.sem, 16 * NTB * b) if b else None)
                fin.append(s_fin.mark(nc.vector.scalar_tensor_tensor(out=r[:], in0=out_tile(n), scalar=gates[:, 1:2],
                                                                     in1=x_sb[:, t, :], op0=ALU.mult, op1=ALU.add)))
                act.need(fin[-1])
                st_o.mark(nc.scalar.dma_start(io["out"].rearrange("(n p) d -> n p d", p=P)[t], r[:]))

        for i in range(len(items) + 1):
            if i < len(items):
                for s in range(NSUB):
                    gate_up(i, s)
            if i > 0:
                down(i - 1)
                if i - 1 + WB < len(items):
                    loaded[i - 1 + WB] = load(i - 1 + WB)
            if i > 0 and items[i - 1][1] == NE - 1:
                finish(items[i - 1][0])
            if i < len(items):
                for s in range(NSUB):
                    hidden(i, s)
        sp.need((st_o.sem, st_o.count), probs_stored)
        act.need((st_o.sem, st_o.count))
        close_scope()


def kernel(x, ctx_2048, g_xattn, g_ffn, L0_xattn_Wq, L0_xattn_bq, L0_xattn_Wkv, L0_xattn_bkv, L0_xattn_Wp,
           L0_xattn_bp, L0_ffn_router_w, L0_ffn_expert_bias, L0_ffn_gate_w, L0_ffn_up_w, L0_ffn_down_w,
           L0_ffn_shared_gate_w, L0_ffn_shared_up_w, L0_ffn_shared_down_w):
    import concourse.bacc as bacc
    from concourse.bass_utils import run_bass_kernel_spmd as run

    n = np.asarray
    D = x.shape[-1]
    bkv = n(L0_xattn_bkv)
    arrays = {
        "x": n(x).reshape(-1, D),
        "ctxT": n(ctx_2048).reshape(-1, D).T,
        "wq": n(L0_xattn_Wq), "wkv": n(L0_xattn_Wkv), "wp": n(L0_xattn_Wp),
        "rows": np.concatenate([n(L0_xattn_bq), bkv[:D], n(L0_xattn_bp), n(g_xattn).reshape(1),
                                n(g_ffn).reshape(1)])[None, :],
        "bv": bkv[D:].reshape(-1, 128).T,
        "router_wT": n(L0_ffn_router_w).T,
        "expert_bias": n(L0_ffn_expert_bias)[None, :],
        "gateT": np.concatenate([n(L0_ffn_gate_w), n(L0_ffn_shared_gate_w)[None]]).transpose(0, 2, 1),
        "upT": np.concatenate([n(L0_ffn_up_w), n(L0_ffn_shared_up_w)[None]]).transpose(0, 2, 1),
        "downT": np.concatenate([n(L0_ffn_down_w), n(L0_ffn_shared_down_w)[None]]).transpose(0, 2, 1),
    }
    arrays = {k: np.ascontiguousarray(a) for k, a in arrays.items()}
    nc = bacc.Bacc("TRN2", target_bir_lowering=False, num_devices=1)
    io = {k: nc.dram_tensor(f"in_{k}", a.shape, mybir.dt.from_np(a.dtype), kind="ExternalInput").ap()
          for k, a in arrays.items()}
    T = arrays["x"].shape[0]
    io["out"] = nc.dram_tensor("out_y", (T, D), F32, kind="ExternalOutput").ap()
    io["prob_scratch"] = nc.dram_tensor("prob_scratch", (arrays["gateT"].shape[0], T), F32, kind="Internal").ap()
    build(nc, io)
    r = run(nc, [{f"in_{k}": a for k, a in arrays.items()}], core_ids=[0])
    return r.results[0]["out_y"].reshape(x.shape)
```

```python
from contextlib import ExitStack

import numpy as np
import concourse.bass as bass
from concourse import mybir

ALU = mybir.AluOpType
ACT = mybir.ActivationFunctionType
AX = mybir.AxisListType
F32 = mybir.dt.float32
BF16 = mybir.dt.bfloat16
F16 = mybir.dt.float16
U8 = mybir.dt.uint8
U16 = mybir.dt.uint16
I32 = mybir.dt.int32
U32 = mybir.dt.uint32

P = 128
ROUND = 1.5 * 2.0 ** 23
OFFSET = 1024.0


class Stage:

    def __init__(self, sem, step=1):
        self.sem, self.step, self.count = sem, step, 0

    def mark(self, instruction):
        instruction.then_inc(self.sem, self.step)
        self.count += self.step
        return self.sem, self.count


class Engine:

    def __init__(self, eng):
        self.eng, self.seen = eng, {}

    def need(self, *steps):
        for step in steps:
            if step is None:
                continue
            sem, value = step
            if self.seen.get(id(sem), 0) < value:
                self.seen[id(sem)] = value
                self.eng.wait_ge(sem, value)
        return self.eng


def build(nc, io):
    T, D = io["x"].shape
    H, HD = 16, D // 16
    E, K = io["router_wT"].shape[1], 4
    I = io["experts"].shape[1] // (E + 1) // (3 * D // P)
    NT, C = T // P, D // P
    PAIRS = H // 2
    REGION = T + P
    NTILE = (T * K - E) // P + E
    BIG = float(2 ** 17)
    SENT = -3.0e38
    FE = 2 * C * I + D
    LN255 = float(np.log(np.float64(255.0)))

    with ExitStack() as ctx:
        scopes = [ctx]

        def sb(name, shape, dt=F32):
            return scopes[-1].enter_context(nc.sbuf_tensor(name, shape, dt))

        def open_scope():
            scopes.append(ExitStack())

        def close_scope():
            scopes.pop().close()

        def stage(name, step=1):
            return Stage(ctx.enter_context(nc.semaphore(name)), step)

        pe, dve, act, pool, sp = (Engine(e) for e in (nc.tensor, nc.vector, nc.scalar, nc.gpsimd, nc.sync))

        x_sb = sb("x_sb", [P, NT, D])
        xn = sb("xn", [P, NT, D])
        wp = sb("wp", [P, C, D])
        rows = sb("rows", [1, 3 * D + 2])
        bv = sb("bv", [P, C])
        wr = sb("wr", [P, C, E])
        eb = sb("eb", [1, E])
        bias_e = sb("bias_e", [P, E])
        x2T = sb("x2T", [P, C, T])
        before = sb("before", [P, P], BF16)
        ones_sq = sb("ones_sq", [P, P], BF16)
        region0 = sb("region0", [P, E])
        key0 = sb("key0", [P, E])
        iota_i = sb("iota_i", [P, E], I32)
        lane_i = sb("lane_i", [P, 1], I32)
        lane = sb("lane", [P, 1])
        token_i = sb("token_i", [P, NT], I32)
        token = sb("token", [P, NT])
        load = sb("load", [P, E], BF16)
        pos_i = sb("pos_i", [P, NT, K], I32)
        score_e = sb("score_e", [P, NT, E])
        keys = sb("keys", [P, NT, E])
        top_keys = sb("top_keys", [P, NT, 8])
        share = sb("share", [P, NT, K])
        ones = sb("ones", [1, P])
        ident = sb("ident", [P, P])
        ident_b = sb("ident_b", [P, P], BF16)
        gates = sb("gates", [P, 2])
        banks = ctx.enter_context(nc.psum_tensor("banks", [P, 8, 512], F32))

        open_scope()
        qT = sb("qT", [P, H, T], BF16)
        kT = sb("kT", [P, PAIRS, T], BF16)
        v_int = sb("v_int", [P, NT, D], BF16)
        v_corr = sb("v_corr", [P, NT // 2, D], F16)
        minus_offset = sb("minus_offset", [P, P], F16)
        sq = sb("sq", [P, NT, H])
        neg_sq = sb("neg_sq", [P, NT, H])
        open_scope()
        wq = sb("wq", [P, C, D])
        wkv = sb("wkv", [P, C, 2 * D])
        xT = sb("xT", [P, C, T])
        cT = x2T
        vT = xn[:].rearrange("p n d -> p (n d)").rearrange("p (c t) -> p c t", c=C)

        ld_x = stage("ld_x", 16)
        ld_w = stage("ld_w", 16)
        ld_c = stage("ld_c", 16)
        ld_l = stage("ld_l", 16)
        got_x = ld_x.mark(nc.sync.dma_start(x_sb[:], io["x"].rearrange("(n p) d -> p n d", p=P)))
        for src, dst in ((io["wq"], wq), (io["wkv"], wkv)):
            got_w = ld_w.mark(nc.sync.dma_start(dst[:], src.rearrange("(c p) d -> p c d", p=P)))
        got_w = ld_w.mark(nc.sync.dma_start(rows[:], io["rows"]))
        got_w = ld_w.mark(nc.sync.dma_start(bv[:], io["bv"]))
        got_c = ld_c.mark(nc.scalar.dma_start(cT[:], io["ctxT"].rearrange("(c p) t -> p c t", p=P)))
        got_l = ld_l.mark(nc.scalar.dma_start(wp[:], io["wp"].rearrange("(c p) d -> p c d", p=P)))
        got_l = ld_l.mark(nc.scalar.dma_start(wr[:], io["router_wT"].rearrange("(c p) e -> p c e", p=P)))
        got_l = ld_l.mark(nc.scalar.dma_start(eb[:], io["expert_bias"]))

        consts = stage("consts")
        made = consts.mark(nc.gpsimd.memset(ident[:], 0.0))
        pool.need(made)
        made = consts.mark(nc.gpsimd.affine_select(out=ident[:], in_=ident[:], compare_op=ALU.not_equal, fill=1.0,
                                                   base=0, pattern=[[-1, P]], channel_multiplier=1))
        pool.need(made)
        consts.mark(nc.gpsimd.tensor_copy(ident_b[:], ident[:]))
        got_const = consts.mark(nc.gpsimd.memset(ones[:], 1.0))
        consts.mark(nc.gpsimd.memset(ones_sq[:], 1.0))
        consts.mark(nc.gpsimd.memset(load[:], 0.0))
        consts.mark(nc.gpsimd.iota(iota_i[:], pattern=[[REGION, E]], base=0, channel_multiplier=0))
        consts.mark(nc.gpsimd.iota(lane_i[:], pattern=[[0, 1]], base=0, channel_multiplier=1))
        consts.mark(nc.gpsimd.iota(token_i[:], pattern=[[P, NT]], base=0, channel_multiplier=1))
        pool.need((consts.sem, consts.count))
        consts.mark(nc.gpsimd.tensor_copy(token[:], token_i[:]))
        consts.mark(nc.gpsimd.tensor_copy(region0[:], iota_i[:]))
        consts.mark(nc.gpsimd.tensor_copy(lane[:], lane_i[:]))
        pool.need((consts.sem, consts.count))
        consts.mark(nc.gpsimd.tensor_scalar(key0[:], region0[:], -1.0, BIG, ALU.mult, ALU.add))
        consts.mark(nc.gpsimd.affine_select(out=before[:], in_=ones_sq[:], compare_op=ALU.is_gt, fill=0.0,
                                            base=0, pattern=[[1, P]], channel_multiplier=-1))
        zeroed = consts.mark(nc.gpsimd.memset(qT[:], 0.0))
        consts.mark(nc.gpsimd.memset(v_corr[:], 0.0))
        consts_all = consts.mark(nc.gpsimd.memset(minus_offset[:], -OFFSET))

        st_e = stage("st_e", 16)
        sp.need(consts_all)
        slots_clear = st_e.mark(nc.sync.dma_start(io["slots"].rearrange("(p n) o -> p (n o)", p=P),
                                                      v_corr[:].rearrange("p n d -> p (n d)").bitcast(F32)[:, 0:E * REGION // P]))

        chain = stage("chain")

        def then(instruction):
            dve.need(chain.mark(instruction))

        root_s = stage("root_s")

        def first_inverse_root(out, var, tmp, y, n):
            then(nc.vector.tensor_scalar(tmp, var, 1e-5, None, ALU.add))
            act.need((chain.sem, chain.count))
            got = root_s.mark(nc.scalar.activation(y, tmp, ACT.Sqrt))
            dve.need(got)
            then(nc.vector.reciprocal(out, y))
            then(nc.vector.tensor_tensor(out, out, tmp, ALU.mult))
            then(nc.vector.tensor_tensor(out, out, y, ALU.add))
            then(nc.vector.tensor_scalar(out, out, 0.5, None, ALU.mult))
            then(nc.vector.reciprocal(out, out))

        stats = sb("stats", [P, NT, 6])
        mv = sb("mv", [P, NT, 2])
        rstd = sb("rstd", [P, NT])
        root_t = sb("root_t", [P, NT])
        root_y = sb("root_y", [P, NT])
        normed = stage("normed")

        def layer_norm():
            for n in range(NT):
                ins = nc.vector.bn_stats(stats[:, n, :], x_sb[:, n, :])
            then(ins)
            for n in range(NT):
                ins = nc.vector.bn_aggr(mv[:, n, :], stats[:, n, :])
            then(ins)
            first_inverse_root(rstd[:], mv[:, :, 1], root_t[:], root_y[:], NT)
            steps = []
            for n in range(NT):
                steps.append(normed.mark(nc.vector.tensor_scalar(xn[:, n, :], x_sb[:, n, :], mv[:, n, 0:1],
                                                                 rstd[:, n:n + 1], ALU.subtract, ALU.mult)))
            return steps

        turned = stage("turned")
        turned_out = stage("turned_out")
        free = {}

        def bank(k):
            return banks[:, k, :]

        def turn(src, dst, ready):
            out = []
            for g in range(NT // 2):
                k = g % 2
                pe.need(got_const, ready[2 * g], ready[2 * g + 1], free.get(k))
                for c in range(C):
                    for n in range(2):
                        ins = nc.tensor.transpose(bank(k)[:, (2 * c + n) * P:(2 * c + n + 1) * P],
                                                  src[:, 2 * g + n, c * P:(c + 1) * P], ident[:])
                got = turned.mark(ins)
                act.need(got)
                step = turned_out.mark(nc.scalar.copy(dst[:, :, 2 * g * P:(2 * g + 2) * P],
                                                      bank(k).rearrange("p (c t) -> p c t", c=C)))
                free[k] = step
                out.append(step)
            return out

        s_gate = stage("s_gate")
        pe.need(got_const, got_w, got_l)
        nc.tensor.matmul(bank(6)[:, 0:2], ones[:], rows[:, 3 * D:3 * D + 2], start=True, stop=True)
        ins = nc.tensor.matmul(bank(6)[:, 2:2 + E], ones[:], eb[:], start=True, stop=True)
        act.need(s_gate.mark(ins))
        s_gate.mark(nc.scalar.copy(bias_e[:], bank(6)[:, 2:2 + E]))
        gate_step = s_gate.mark(nc.scalar.activation(gates[:], bank(6)[:, 0:2], ACT.Tanh))
        free[6] = gate_step

        proj = stage("proj")
        q4 = sb("q4", [P, 2, 2, H, 4, HD], BF16)
        quant0 = sb("quant0", [P, 2, H, HD])
        kfull0 = sb("kfull0", [P, 2, H, HD])
        quant = [quant0[:], keys[:].rearrange("p n e -> p (n e)").rearrange("p (n h d) -> p n h d", n=2, h=H)]
        kfull = [kfull0[:], score_e[:].rearrange("p n e -> p (n e)").rearrange("p (n h d) -> p n h d", n=2, h=H)]
        amax = sb("amax", [P, 2, H])
        rec = sb("rec", [P, 2, H])
        sk = sb("sk", [P, 2, 2, H])
        then(nc.vector.memset(q4[:], 0.0))
        in_setup = {"dve": chain, "pool": stage("setup_pool"), "act": stage("setup_act")}
        turn4 = stage("turn4")
        sums_s = stage("sums_s")
        items = [("k", g) for g in range(NT // 2)] + [("q", g) for g in range(NT // 2)]
        q4_read, cut_done, projected = {}, {}, {}
        SLOT_BANKS = 4

        def did(name, instruction):
            return in_setup[name].mark(instruction)

        def project(n):
            what, g = items[n]
            k = (n + 2) % SLOT_BANKS
            row, w, src, src_step = (1, wkv, cT, got_c) if what == "k" else (0, wq, xT, xT_steps[g])
            pe.need(src_step, got_w, got_const, free.get(k))
            for m in range(2):
                o = bank(k)[:, m * D:(m + 1) * D]
                for c in range(C):
                    nc.tensor.matmul(o, src[:, c, (2 * g + m) * P:(2 * g + m + 1) * P], w[:, c, 0:D], start=(c == 0), stop=False)
                ins = nc.tensor.matmul(o, ones[:], rows[:, row * D:(row + 1) * D], start=False, stop=True)
            projected[n] = proj.mark(ins)

        def quantise(n):
            what, g = items[n]
            k, b = (n + 2) % SLOT_BANKS, n % 2
            x = quant[b]
            ps = bank(k).rearrange("p (n h d) -> p n h d", n=2, h=H)
            s = sk[:, b] if what == "k" else sq[:, 2 * g:2 * g + 2, :]
            scale = 1.0 if what == "k" else 0.25
            dve.need(projected[n], cut_done.get(n - 2))
            then(nc.vector.tensor_reduce(amax[:], ps, AX.X, ALU.max, apply_absolute_value=True))
            then(nc.vector.tensor_scalar(s, amax[:], scale / 127.0, 1e-8, ALU.mult, ALU.max))
            then(nc.vector.reciprocal(rec[:], s))
            if scale != 1.0:
                then(nc.vector.tensor_scalar(rec[:], rec[:], scale, None, ALU.mult))
            free[k] = a = did("dve", nc.vector.tensor_tensor(x, ps, rec[:].unsqueeze(3).broadcast_to([P, 2, H, HD]), ALU.mult))
            dve.need(a)
            then(nc.vector.tensor_scalar(x, x, 127.0, -127.0, ALU.min, ALU.max))
            if what == "q":
                dve.need(q4_read.get(n - 2))
                x = q4[:, b, :, :, 0, :]
            whole[n] = did("dve", nc.vector.tensor_scalar(x, quant[b], ROUND, ROUND, ALU.add, ALU.subtract))

        def fill_slots(n):
            what, g = items[n]
            b = n % 2
            x = quant[b]
            hi, mid, lo = (q4[:, b, :, :, j, :] for j in range(3))
            if what == "q":
                pool.need(whole[n])
                did("pool", nc.gpsimd.tensor_copy(mid, hi))
                cut_done[n] = did("pool", nc.gpsimd.tensor_copy(lo, hi))
                return
            pool.need(whole[n])
            a = did("pool", nc.gpsimd.tensor_tensor(kfull[b], x, sk[:, b].unsqueeze(3).broadcast_to([P, 2, H, HD]), ALU.mult))
            act.need(a, q4_read.get(n - 2))
            a = did("act", nc.scalar.copy(hi, kfull[b]))
            pool.need(a)
            a = did("pool", nc.gpsimd.tensor_tensor(x, kfull[b], hi, ALU.subtract))
            act.need(a)
            a = did("act", nc.scalar.copy(mid, x))
            pool.need(a)
            cut_done[n] = did("pool", nc.gpsimd.tensor_tensor(lo, x, mid, ALU.subtract))

        whole = {}

        def turn_item(n):
            what, g = items[n]
            b = n % 2
            for m in range(2):
                k2 = 4 + m
                t0 = (2 * g + m) * P
                pe.need(cut_done[n], *free.get(k2, ()))
                tb = bank(k2).bitcast(BF16)
                for pair in range(PAIRS):
                    ins = nc.tensor.transpose(tb[:, pair * P:(pair + 1) * P],
                                              q4[:, b, m, 2 * pair:2 * pair + 2, :, :].rearrange("p h s d -> p (h s d)"),
                                              ident_b[:])
                a = turn4.mark(ins)
                q4_read[n] = a
                act.need(a)
                tb = tb.rearrange("p (c t) -> p c t", c=PAIRS)
                if what == "k":
                    free[k2] = (did("act", nc.scalar.copy(kT[:, :, t0:t0 + P], tb)),)
                elif m == 0:
                    act.need(*zeroed_all)
                    did("act", nc.scalar.copy(qT[0:64, 0:H:2, t0:t0 + P], tb[0:64]))
                    free[k2] = (did("act", nc.scalar.copy(qT[64:P, 1:H:2, t0:t0 + P], tb[64:P])),)
                else:
                    act.need(*zeroed_all)
                    x1 = did("act", nc.scalar.copy(qT[0:64, 0:H:2, t0:t0 + P], tb[0:64]))
                    dve.need(a, *zeroed_all)
                    free[k2] = (x1, did("dve", nc.vector.tensor_copy(qT[64:P, 1:H:2, t0:t0 + P], tb[64:P])))

        vproj = stage("vproj")
        vout = stage("vout")
        vmax = sb("vmax", [P, C])
        sv = sb("sv", [P, C])
        rv = sb("rv", [P, C])
        vTi = qT[:, H - 2:H, :]
        ones_b = sb("ones_b", [P, 2], BF16)

        def project_v():
            for c in range(C):
                for t in range(T // 512):
                    k = 6 + t % 2
                    pe.need(free.get(k), got_w, got_c)
                    for d in range(C):
                        ins = nc.tensor.matmul(bank(k), wkv[:, d, D + c * P:D + (c + 1) * P],
                                               cT[:, d, t * 512:(t + 1) * 512], start=(d == 0), stop=(d == C - 1))
                    act.need(vproj.mark(ins), (turned.sem, turned.count))
                    free[k] = vout.mark(nc.scalar.activation(vT[:, c, t * 512:(t + 1) * 512], bank(k), ACT.Identity,
                                                             bias=bv[:, c:c + 1]))

        def quantise_v():
            dve.need((vout.sem, vout.count))
            then(nc.vector.tensor_reduce(vmax[:], vT, AX.X, ALU.max, apply_absolute_value=True))
            then(nc.vector.tensor_scalar(sv[:], vmax[:], 1.0 / 127.0, 1e-8, ALU.mult, ALU.max))
            then(nc.vector.reciprocal(rv[:], sv[:]))
            for c in range(C):
                ins = nc.vector.tensor_scalar(vT[:, c, :], vT[:, c, :], rv[:, c:c + 1], 127.0, ALU.mult, ALU.min)
            then(ins)
            then(nc.vector.tensor_scalar(vT, vT, -127.0, ROUND, ALU.max, ALU.add))
            dve.need(zeroed)
            then(nc.vector.tensor_scalar(vTi, vT, ROUND, None, ALU.subtract))

        def turn_v(g):
            k = 6 + g % 2
            pe.need(v_round, free.get(k))
            tb = bank(k).bitcast(BF16)
            for n in range(4):
                for c in range(C):
                    ins = nc.tensor.transpose(tb[:, (2 * n + c) * P:(2 * n + c + 1) * P],
                                              vTi[:, c, (4 * g + n) * P:(4 * g + n + 1) * P], ident_b[:])
            act.need(turn4.mark(ins))
            free[k] = did("act", nc.scalar.copy(v_int[:, 4 * g:4 * g + 4, :], tb.rearrange("p (n d) -> p n d", n=4)))

        vs_hi = vT[0:2, 0, 0:D].bitcast(F16)
        vs_lo = vT[0:2, 1, 0:2 * D]

        def sum_v(g):
            k = 6 + g % 2
            pe.need(free.get(k))
            for n in range(4):
                ins = nc.tensor.matmul(bank(k)[0:2, (n // 2) * D:(n // 2 + 1) * D], ones_b[:], v_int[:, 4 * g + n, :],
                                       start=(n % 2 == 0), stop=(n % 2 == 1))
            dve.need(sums_s.mark(ins))
            sums = bank(k)[0:2, :]
            then(nc.vector.tensor_copy(vs_hi, sums))
            then(nc.vector.tensor_tensor(vs_lo, sums, vs_hi, ALU.subtract))
            free[k] = (chain.sem, chain.count)
            then(nc.vector.tensor_scalar(vs_lo, vs_lo, ident[0:2, 1:2], None, ALU.mult))
            then(nc.vector.scalar_tensor_tensor(out=v_corr[0:2, 2 * g:2 * g + 2, :].rearrange("p n d -> p (n d)"),
                                                in0=vs_hi, scalar=ident[0:2, 0:1], in1=vs_lo,
                                                op0=ALU.mult, op1=ALU.add))

        zeroed_all = [zeroed]
        then(nc.vector.memset(ones_b[:], 1.0))
        for n in range(2):
            project(n)
        dve.need(got_x)
        steps = layer_norm()
        xT_steps = turn(xn, xT, steps)
        project_v()
        dve.need(got_l)
        for n in range(len(items)):
            if n + 2 < len(items):
                project(n + 2)
            quantise(n)
            if n == 1:
                quantise_v()
                v_round = (chain.sem, chain.count)
                for c in range(C):
                    ins = nc.vector.tensor_scalar(wp[:, c, :], wp[:, c, :], sv[:, c:c + 1], None, ALU.mult)
                then(ins)
                wp_scaled = (chain.sem, chain.count)
            if 2 <= n < 2 + NT // 4:
                turn_v(n - 2)
                if n == 1 + NT // 4:
                    pool.need((turn4.sem, turn4.count))
                    zeroed_all.append(did("pool", nc.gpsimd.memset(vTi, 0.0)))
                    pe.need((in_setup["act"].sem, in_setup["act"].count))
                    dve.need(got_const, consts_all, slots_clear)
            if 2 + NT // 4 <= n < 2 + NT // 2:
                sum_v(n - 2 - NT // 4)
            if n > 0:
                turn_item(n - 1)
            fill_slots(n)
        turn_item(len(items) - 1)
        then(nc.vector.tensor_scalar(neg_sq[:], sq[:], -1.0, None, ALU.mult))
        setup_over = [(in_setup[e].sem, in_setup[e].count) for e in ("dve", "pool", "act")]
        k_ready = q_ready = v_ready = setup_over[2]
        v_ready2 = setup_over[0]

        close_scope()
        NB = 4
        NW = 3
        words = sb("words", [P, NW, T], U16)
        pT = sb("pT", [P, NB, NT, P], F16)
        MR = 8
        hmax = sb("hmax", [P, MR, 4])
        umax = sb("umax", [P, MR])
        nb_t = sb("nb_t", [P, MR])
        nbias = sb("nbias", [P, MR])
        psums = sb("psums", [P, NT, H, 2])
        norm = sb("norm", [P, NT, H])
        pool.need(*setup_over)
        filled = consts.mark(nc.gpsimd.memset(words[:], 0x6400))
        free.clear()
        heads_out = xn

        s_mm, s_max, s_two, s_neg, s_bias, s_exp = (stage(n) for n in ("s_mm", "s_max", "s_two", "s_neg", "s_bias", "s_exp"))
        s_sc, s_pv = stage("s_sc"), stage("s_pv")
        s_turn = [stage(f"s_turn{n}", 16) for n in range(NB)]
        U = NT * H
        scored, maxd, scored2, expd, turnd, pvd, biasd, normd = ({} for _ in range(8))
        bytes_of = words[:].bitcast(U8).rearrange("p b (t two) -> p b t two", two=2)
        word_f16 = words[:].bitcast(F16)

        def score(out, u, k0):
            t, h = divmod(u, H)
            return nc.tensor.matmul(out, qT[:, h, t * P:(t + 1) * P], kT[:, h // 2, k0:k0 + 512], start=True, stop=True)

        def do_scores_max(u, m):
            j = 4 * u + m
            pe.need(*setup_over, maxd.get(j - 2), free.get(j % 2))
            scored[j] = s_mm.mark(score(bank(j % 2), u, m * 512))

        def do_max(u, m):
            j = 4 * u + m
            dve.need(scored[j], biasd.get(u - MR))
            maxd[j] = s_max.mark(nc.vector.tensor_reduce(hmax[:, u % MR, m:m + 1], bank(j % 2), AX.X, ALU.max))

        def do_bias(u):
            t, h = divmod(u, H)
            r = u % MR
            two = slice(r, r + 2)
            dve.need(maxd[4 * u + 7], biasd.get(u - MR))
            pool.need(s_two.mark(nc.vector.tensor_reduce(umax[:, two], hmax[:, two, :], AX.X, ALU.max)))
            pool.need(expd.get(2 * (u + 1 - MR) + 1), q_ready)
            pool.need(s_neg.mark(nc.gpsimd.tensor_tensor(nb_t[:, two], umax[:, two], neg_sq[:, t, h:h + 2], ALU.mult)))
            biasd[u] = biasd[u + 1] = s_bias.mark(nc.gpsimd.tensor_scalar(nbias[:, two], nb_t[:, two], LN255, None, ALU.add))

        def do_scores_exp(u, half):
            j = 2 * u + half
            pe.need(expd.get(j - 2), free.get(3 + 2 * (j % 2)), free.get(4 + 2 * (j % 2)))
            for m in range(2):
                ins = score(bank(3 + 2 * (j % 2) + m), u, (2 * half + m) * 512)
            scored2[j] = s_sc.mark(ins)

        def do_exp(u, half):
            t, h = divmod(u, H)
            j = 2 * u + half
            b0 = 3 + 2 * (j % 2)
            act.need(scored2[j], biasd[u], filled, turnd.get(u - NW))
            expd[j] = s_exp.mark(nc.scalar.activation(
                bytes_of[:, u % NW, half * (T // 2):(half + 1) * (T // 2), 0:1],
                banks[:, b0:b0 + 2, :].rearrange("p m (n o) -> p (m n) o", o=1), ACT.Exp,
                bias=nbias[:, u % MR:u % MR + 1], scale=sq[:, t, h:h + 1], accum_out=psums[:, t, h, half:half + 1]))

        def do_turn(u):
            sp.need(expd[2 * u + 1], pvd.get(u - NB))
            turnd[u] = s_turn[u % NB].mark(nc.sync.dma_start_transpose(pT[:, u % NB, :, :], word_f16[:, u % NW, :]))

        def do_pv(u, half):
            t, h = divmod(u, H)
            cols = slice(h * HD, (h + 1) * HD)
            pe.need(turnd[u], v_ready, v_ready2, normd.get(t - 1))
            for kt in range(half * NT // 2, (half + 1) * NT // 2):
                ins = nc.tensor.matmul(bank(7)[:, cols], pT[:, u % NB, kt, :], v_int[:, kt, cols],
                                       start=(kt == 0), stop=(kt == NT - 1))
                if kt % 2 == 0:
                    nc.tensor.matmul(bank(7)[:, cols], minus_offset[:], v_corr[:, kt // 2, cols], start=False, stop=False)
            step = s_pv.mark(ins)
            if half == 1:
                pvd[u] = step

        by = {name: stage(f"by_{name}") for name in ("pe", "dve", "act", "pool")}
        queue = {"pe": pe, "dve": dve, "act": act, "pool": pool}

        def does(name, instruction):
            return by[name].mark(instruction)

        hT_t = sb("hT_t", [P, C, P])
        stat = sb("stat", [P, 6])
        mean_var = sb("mean_var", [P, 2])
        small = sb("small", [P, 8])
        logit = sb("logit", [P, E])
        relu = sb("relu", [P, E])
        w1, w2, w3, w4 = (sb(f"w{n}", [P, E]) for n in range(1, 5))
        choose = sb("choose", [P, E + 8])
        chosen = sb("chosen", [P, E + 8])
        top = sb("top", [P, 8])
        top4 = sb("top4", [P, 8])
        mask_b = sb("mask_b", [P, E], BF16)
        consts.mark(nc.gpsimd.memset(choose[:], SENT))
        fillers = consts.mark(nc.gpsimd.memset(top4[:], SENT))
        st_x = stage("st_x", 16)
        st_xn = stage("st_xn", 16)
        post_bank = bank(2)
        half_a, half_b = post_bank[:, 0:D], post_bank[:, D:2 * D]

        def do_norm_scale(t):
            n = norm[:, t, :]
            pool.need(expd[2 * (t * H + H - 1) + 1])
            dve.need(does("pool", nc.gpsimd.tensor_tensor(n, psums[:, t, :, 0], psums[:, t, :, 1], ALU.add)))
            pool.need(does("dve", nc.vector.reciprocal(n, n)))
            normd[t] = does("pool", nc.gpsimd.tensor_scalar(n, n, 1e-8, None, ALU.max))

        def do_norm(t):
            dve.need(normd[t], pvd[t * H + H - 1])
            normd[t] = does("dve", nc.vector.tensor_tensor(
                heads_out[:, t, :].rearrange("p (h d) -> p h d", h=H), bank(7)[:, 0:D].rearrange("p (h d) -> p h d", h=H),
                norm[:, t, :].unsqueeze(2).broadcast_to([P, H, HD]), ALU.mult))

        def later(steps):
            for _ in range(steps):
                yield

        def pool_ops(*instructions):
            for make in instructions:
                step = does("pool", make())
                pool.need(step)
            return step

        def inverse_root(x, y, t1, x_step):
            dve.need(x_step)
            a = does("dve", nc.vector.tensor_scalar(y.bitcast(I32), x.bitcast(I32), 1, None, ALU.arith_shift_right))
            yield
            pool.need(a)
            pool_ops(lambda: nc.gpsimd.tensor_scalar(y.bitcast(I32), y.bitcast(I32), -1.0, float(0x5f3759df),
                                                     ALU.mult, ALU.add))
            yield
            for _ in range(3):
                pool_ops(lambda: nc.gpsimd.tensor_tensor(t1, y, y, ALU.mult),
                         lambda: nc.gpsimd.tensor_tensor(t1, t1, x, ALU.mult))
                yield
                a = pool_ops(lambda: nc.gpsimd.tensor_scalar(t1, t1, -0.5, 1.5, ALU.mult, ALU.add),
                             lambda: nc.gpsimd.tensor_tensor(y, y, t1, ALU.mult))
                yield
            return a

        bank2 = {"written": None, "read": free.get(2)}

        def write_bank2(*instructions, last=True):
            pe.need(bank2["read"])
            for make in instructions:
                ins = make()
            bank2["written"] = does("pe", ins)
            return bank2["written"]

        def read_bank2(name, make):
            queue[name].need(bank2["written"])
            bank2["read"] = does(name, make())
            return bank2["read"]

        def close_layer(t):
            xt = x_sb[:, t, :]
            ts = slice(t * P, (t + 1) * P)
            yield from later(2)
            pe.need(normd[t])
            write_bank2(*(lambda c=c: nc.tensor.transpose(half_a[:, c * P:(c + 1) * P], heads_out[:, t, c * P:(c + 1) * P],
                                                          ident[:]) for c in range(C)))
            yield
            a = read_bank2("act", lambda: nc.scalar.copy(hT_t[:].rearrange("p c t -> p (c t)"), half_a))
            yield from later(3)
            pe.need(a, wp_scaled)
            for c in range(C):
                write_bank2(lambda: nc.tensor.matmul(half_a, hT_t[:, c, :], wp[:, c, :], start=(c == 0), stop=False))
                projecting[0] = True
                yield
            write_bank2(lambda: nc.tensor.matmul(half_a, ones[:], rows[:, 2 * D:3 * D], start=False, stop=True))
            projecting[0] = False
            yield
            dve.need(gate_step)
            a = read_bank2("dve", lambda: nc.vector.scalar_tensor_tensor(out=xt, in0=half_a, scalar=gates[:, 0:1],
                                                                         in1=xt, op0=ALU.mult, op1=ALU.add))
            yield
            dve.need(a)
            a = does("dve", nc.vector.bn_stats(stat[:], xt))
            yield
            dve.need(a)
            a = does("dve", nc.vector.bn_aggr(mean_var[:], stat[:]))
            yield
            v, r, t1 = small[:, 0:1], small[:, 1:2], small[:, 2:3]
            pool.need(a)
            a = pool_ops(lambda: nc.gpsimd.tensor_scalar(v, mean_var[:, 1:2], 1e-5, None, ALU.add))
            yield from later(2)
            a = yield from inverse_root(v, r, t1, a)
            yield from later(3)
            dve.need(a)
            a = does("dve", nc.vector.tensor_scalar(xn[:, t, :], xt, mean_var[:, 0:1], r, ALU.subtract, ALU.mult))
            sp.need(a)
            st_xn.mark(nc.sync.dma_start(io["x_norm"][t * P:(t + 1) * P, :], xn[:, t, :]))
            yield from later(3)
            pe.need(a)
            write_bank2(*(lambda c=c: nc.tensor.transpose(half_a[:, c * P:(c + 1) * P], xn[:, t, c * P:(c + 1) * P],
                                                          ident[:]) for c in range(C)))
            yield
            a = x2T_ready[t] = read_bank2("act", lambda: nc.scalar.copy(
                x2T[:, :, ts], half_a.rearrange("p (c t) -> p c t", c=C)))
            yield from later(3)
            pe.need(a)
            write_bank2(*(lambda c=c: nc.tensor.matmul(half_a[:, 0:E], x2T[:, c, ts], wr[:, c, :], start=(c == 0),
                                                       stop=(c == C - 1)) for c in range(C)))
            yield
            dve.need(logit_read[0])
            logit_ready[t] = read_bank2("dve", lambda: nc.vector.tensor_copy(logit[:], half_a[:, 0:E]))
            yield

        def choose_experts(t):
            dve.need(logit_ready[t])
            a = does("dve", nc.vector.scalar_tensor_tensor(out=w1[:], in0=logit[:], scalar=-1.0, in1=logit[:],
                                                           op0=ALU.mult, op1=ALU.min))
            pool.need(logit_ready[t])
            positive = logit_read[0] = pool_ops(lambda: nc.gpsimd.tensor_scalar(relu[:], logit[:], 0.0, None, ALU.max))
            yield from later(2)
            act.need(a)
            a = does("act", nc.scalar.activation(w2[:], w1[:], ACT.Exp))
            yield from later(3)
            pool.need(a)
            a = pool_ops(lambda: nc.gpsimd.tensor_scalar(w3[:], w2[:], 2.0, None, ALU.add))
            yield from later(2)
            dve.need(a)
            a = does("dve", nc.vector.reciprocal(w3[:], w3[:]))
            yield
            pool.need(a)
            pool_ops(lambda: nc.gpsimd.tensor_tensor(w3[:], w3[:], w2[:], ALU.mult),
                     lambda: nc.gpsimd.tensor_tensor(w4[:], w3[:], w3[:], ALU.mult))
            yield
            pool_ops(lambda: nc.gpsimd.tensor_scalar(w1[:], w4[:], 1 / 15, 1 / 13, ALU.mult, ALU.add))
            for m in (11, 9, 7, 5, 3, 1):
                pool_ops(lambda: nc.gpsimd.tensor_tensor(w1[:], w1[:], w4[:], ALU.mult),
                         lambda: nc.gpsimd.tensor_scalar(w1[:], w1[:], 1 / m, None, ALU.add))
                yield
            pool_ops(lambda: nc.gpsimd.tensor_tensor(w1[:], w1[:], w3[:], ALU.mult),
                     lambda: nc.gpsimd.tensor_scalar(w1[:], w1[:], 2.0, None, ALU.mult))
            yield
            a = pool_ops(lambda: nc.gpsimd.tensor_tensor(w1[:], w1[:], relu[:], ALU.add))
            yield from later(3)
            a = yield from inverse_root(w1[:], w2[:], w4[:], a)
            pool.need(fillers, gate_step)
            a = pool_ops(lambda: nc.gpsimd.tensor_tensor(score_e[:, t, :], w2[:], w1[:], ALU.mult),
                         lambda: nc.gpsimd.tensor_tensor(choose[:, 0:E], score_e[:, t, :], bias_e[:], ALU.add))
            yield from later(3)
            dve.need(a)
            a = does("dve", nc.vector.max(top[:], choose[:]))
            yield
            pool.need(a)
            a = pool_ops(lambda: nc.gpsimd.tensor_copy(top4[:, 0:K], top[:, 0:K]))
            yield from later(2)
            dve.need(a)
            a = does("dve", nc.vector.match_replace(chosen[:], top4[:], choose[:], SENT))
            yield
            pool.need(a)
            a = pool_ops(lambda: nc.gpsimd.tensor_scalar(mask_b[:], chosen[:, 0:E], SENT, None, ALU.is_equal))
            yield from later(4)
            while projecting[0]:
                yield
            pe.need(a)
            ranked = write_bank2(lambda: nc.tensor.matmul(half_b[:, 0:E], before[:], mask_b[:], start=True, stop=False),
                                 lambda: nc.tensor.matmul(half_b[:, 0:E], ones_sq[:], load[:], start=False, stop=True))
            a = read_bank2("dve", lambda: nc.vector.scalar_tensor_tensor(
                out=keys[:, t, :], in0=half_b[:, 0:E], scalar=-1.0, in1=key0[:], op0=ALU.mult, op1=ALU.add))
            yield
            pool.need(a, ranked)
            a = does("pool", nc.gpsimd.tensor_tensor(keys[:, t, :], keys[:, t, :], mask_b[:], ALU.mult))
            does("pool", nc.gpsimd.tensor_tensor(load[:], load[:], mask_b[:], ALU.add))
            yield from later(2)
            dve.need(a)
            a = does("dve", nc.vector.max(top_keys[:, t, :], keys[:, t, :]))
            yield
            pool.need(a)
            pool_ops(lambda: nc.gpsimd.tensor_scalar(pos_i[:, t, :], top_keys[:, t, 0:K], -1.0, BIG, ALU.mult, ALU.add))
            yield
            pool.need(slots_clear)
            for k in range(K):
                st_x.mark(nc.gpsimd.indirect_dma_start(
                    out=io["slots"], out_offset=bass.IndirectOffsetOnAxis(ap=pos_i[:, t, k:k + 1].bitcast(U32), axis=0),
                    in_=token[:, t:t + 1], in_offset=None))
                yield from later(2)

        projecting, logit_read, logit_ready = [False], [None], {}

        def by_now(name):
            return by[name].sem, by[name].count

        x2T_ready = {}

        to_close, to_route = [], []

        def advance():
            if to_close and next(to_close[0][1], "over") == "over":
                t, _ = to_close.pop(0)
                to_route.append(choose_experts(t))
            if to_route and next(to_route[0], "over") == "over":
                to_route.pop(0)

        LAG_X, LAG_V = 3, 6
        for i in range(U + LAG_V):
            a, v = i - LAG_X, i - LAG_V
            for half in range(2):
                if i < U:
                    do_scores_max(i, 2 * half)
                    do_max(i, 2 * half)
                if 0 <= a < U:
                    do_scores_exp(a, half)
                    do_exp(a, half)
                advance()
                if i < U:
                    do_scores_max(i, 2 * half + 1)
                    do_max(i, 2 * half + 1)
                if v >= 0:
                    do_pv(v, half)
                if v >= 0 and v % H == H - 1:
                    do_norm_scale(v // H) if half == 0 else do_norm(v // H)
                if half == 0:
                    advance()
            if i < U and i % 2 == 1:
                do_bias(i - 1)
            if 0 <= a < U:
                do_turn(a)
            if v >= 0 and v % H == H - 1:
                to_close.append((v // H, close_layer(v // H)))
            advance()
        while to_close or to_route:
            advance()

        close_scope()
        open_scope()
        over = (by_now("pe"), by_now("dve"), by_now("act"), by_now("pool"), expd[2 * U - 1])
        for k in range(8):
            free[k] = None
        W = sb("W", [P, E + 1, FE])
        ld_shared = stage("ld_shared", 16)
        ld_exp = stage("ld_exp", 16)
        sp.need(*over)
        sp.need(turnd[U - 1], pvd[U - 1])
        got_shared = ld_shared.mark(nc.sync.dma_start(W[:, E, :], io["experts"][:, E * FE:(E + 1) * FE]))
        for g in range(4):
            e0, e1 = g * E // 4, (g + 1) * E // 4
            got_exp = ld_exp.mark(nc.sync.dma_start(W[:, e0:e1, :].rearrange("p e f -> p (e f)"),
                                                    io["experts"][:, e0 * FE:e1 * FE]))
        count = sb("count", [P, E])
        ntile = sb("ntile", [P, E])
        ends = [sb(f"ends{n}", [P, E]) for n in range(2)]
        le = sb("le", [P, E])
        tmp = sb("tmp", [P, E])
        tile_no = sb("tile_no", [P, 1])
        e_t = sb("e_t", [P, 1])
        first = sb("first", [P, 1])
        first_i = sb("first_i", [P, 1], I32)
        lists = sb("lists", [P, P])
        s1 = sb("s1", [P, 2])
        spread = sb("spread", [P, P])
        rows_i = sb("rows_i", [P, P], I32)
        expert_i = sb("expert_i", [1, P], I32)
        ones_f = sb("ones_f", [P, P])
        pe.need(*over)
        dve.need(*over)
        act.need(*over)
        counted = does("pe", nc.tensor.matmul(bank(0)[:, 0:E], ones_sq[:], load[:], start=True, stop=True))
        dve.need(counted)
        then(nc.vector.memset(ones_f[:], 1.0))
        then(nc.vector.tensor_copy(count[:], bank(0)[:, 0:E]))
        then(nc.vector.tensor_scalar(tmp[:], count[:], float(P - 1), 1.0 / P, ALU.add, ALU.mult))
        then(nc.vector.tensor_scalar(tmp[:], tmp[:], 0.5 - 0.5 / P, ROUND, ALU.subtract, ALU.add))
        then(nc.vector.tensor_scalar(ntile[:], tmp[:], ROUND, None, ALU.subtract))
        then(nc.vector.tensor_copy(ends[0][:], ntile[:]))
        step, q = 1, 0
        while step < E:
            nc.vector.tensor_copy(ends[1 - q][:, 0:step], ends[q][:, 0:step])
            then(nc.vector.tensor_tensor(ends[1 - q][:, step:E], ends[q][:, step:E], ends[q][:, 0:E - step], ALU.add))
            step, q = 2 * step, 1 - q
        end = ends[q]
        then(nc.vector.tensor_scalar(s1[:, 0:1], end[:, E - 1:E], -1.0, None, ALU.add))
        then(nc.vector.tensor_scalar(tile_no[:], lane[:], s1[:, 0:1], None, ALU.min))
        then(nc.vector.tensor_scalar(le[:], end[:], tile_no[:], None, ALU.is_le))
        then(nc.vector.tensor_reduce(e_t[:], le[:], AX.X, ALU.add))
        then(nc.vector.tensor_tensor(tmp[:], le[:], end[:], ALU.mult))
        then(nc.vector.tensor_reduce(s1[:, 1:2], tmp[:], AX.X, ALU.max))
        then(nc.vector.tensor_scalar(first[:], tile_no[:], s1[:, 1:2], None, ALU.subtract))
        then(nc.vector.tensor_scalar(s1[:, 0:1], e_t[:], float(REGION // P), None, ALU.mult))
        then(nc.vector.tensor_scalar(first_i[:], first[:], s1[:, 0:1], None, ALU.add))
        first_ready = (chain.sem, chain.count)
        then(nc.vector.tensor_scalar(spread[:], ident[:], e_t[:], None, ALU.mult))
        ld_list = stage("ld_list", 16)
        pool.need((st_x.sem, st_x.count), first_ready)
        got_list = ld_list.mark(nc.gpsimd.indirect_dma_start(
            out=lists[:], out_offset=None, in_=io["slots"].rearrange("(r p) o -> r (p o)", p=P),
            in_offset=bass.IndirectOffsetOnAxis(ap=first_i[:, 0:1].bitcast(U32), axis=0)))
        pe.need((chain.sem, chain.count))
        a = does("pe", nc.tensor.matmul(bank(1)[:, 0:P], ones_f[:], spread[:], start=True, stop=True))
        dve.need(a)
        then(nc.vector.tensor_copy(expert_i[:], bank(1)[0:1, 0:P]))
        expert_ready = (chain.sem, chain.count)
        pe.need(got_list)
        a = does("pe", nc.tensor.transpose(bank(0)[:, 0:P], lists[:], ident[:]))
        dve.need(a)
        then(nc.vector.tensor_copy(rows_i[:], bank(0)[:, 0:P]))
        rows_ready = (chain.sem, chain.count)
        shift = sb("shift", [P, E])
        pick = sb("pick", [P, NT, K, E])
        moved = sb("moved", [P, NT, K, E])
        weight = sb("weight", [P, NT, E])
        total = sb("total", [P, NT])
        y_f = sb("y_f", [P, NT, K])
        y_i = sb("y_i", [P, NT * K], I32)
        over_k = [P, NT, K, E]
        top_k = top_keys[:, :, 0:K]
        then(nc.vector.tensor_tensor(shift[:], end[:], ntile[:], ALU.subtract))
        then(nc.vector.tensor_scalar(shift[:], shift[:], float(P), None, ALU.mult))
        then(nc.vector.tensor_tensor(shift[:], shift[:], region0[:], ALU.subtract))
        then(nc.vector.tensor_tensor(pick[:], keys[:].unsqueeze(2).broadcast_to(over_k),
                                     top_k.unsqueeze(3).broadcast_to(over_k), ALU.is_equal))
        then(nc.vector.tensor_tensor(moved[:].rearrange("p n k e -> p (n k) e"), pick[:].rearrange("p n k e -> p (n k) e"),
                                     shift[:].unsqueeze(1).broadcast_to([P, NT * K, E]), ALU.mult))
        then(nc.vector.tensor_reduce(y_f[:], moved[:], AX.X, ALU.add))
        then(nc.vector.tensor_tensor(y_f[:], y_f[:], top_k, ALU.subtract))
        then(nc.vector.tensor_scalar(y_i[:], y_f[:].rearrange("p n k -> p (n k)"), BIG, None, ALU.add))
        y_ready = (chain.sem, chain.count)

        def weigh():
            then(nc.vector.tensor_scalar(weight[:], keys[:], 0.0, None, ALU.is_gt))
            then(nc.vector.tensor_tensor(weight[:], weight[:], score_e[:], ALU.mult))
            then(nc.vector.tensor_reduce(total[:], weight[:], AX.X, ALU.add))
            then(nc.vector.tensor_scalar(total[:], total[:], 1e-20, None, ALU.add))
            then(nc.vector.reciprocal(total[:], total[:]))
            then(nc.vector.tensor_scalar(total[:], total[:], 0.5, gates[:, 1:2], ALU.mult, ALU.mult))
            then(nc.vector.tensor_tensor(weight[:], weight[:], total[:].unsqueeze(2).broadcast_to([P, NT, E]), ALU.mult))
            then(nc.vector.tensor_tensor(moved[:], pick[:], weight[:].unsqueeze(2).broadcast_to(over_k), ALU.mult))
            then(nc.vector.tensor_reduce(share[:], moved[:], AX.X, ALU.add))

        weigh()

        J = NT + NTILE
        NX = 4
        xg = sb("xg", [P, NX, D])
        xgT = sb("xgT", [P, 3, C, P])
        R = 4
        gu = sb("gu", [P, R, 2 * I])
        th = sb("th", [P, R, I])
        hid = sb("hid", [P, R, I])
        hidT = sb("hidT", [I, R, P])
        NY = 3
        y_sb = sb("y_sb", [P, NY, D])
        half_gate = sb("half_gate", [P, 1])
        then(nc.vector.tensor_scalar(half_gate[:], gates[:, 1:2], 0.5, None, ALU.mult))
        ld_xg = [stage(f"ld_xg{n}", 16) for n in range(NX)]
        st_y = [stage(f"st_y{n}", 16) for n in range(NY)]
        names = ("t_turn", "t_copy", "t_gu", "t_clip", "t_tanh", "t_gate", "t_hid", "t_hturn", "t_hcopy", "t_down", "t_out")
        st = {n: stage(n) for n in names}
        done = {n: {} for n in names}
        fetched, stored = {}, {}
        pool.need((st_xn.sem, st_xn.count), rows_ready)

        def mark(name, j, ins):
            done[name][j] = st[name].mark(ins)

        def fetch(j):
            if j >= NT:
                g = j - NT
                pool.need(done["t_turn"].get(j - NX))
                fetched[j] = ld_xg[g % NX].mark(nc.gpsimd.indirect_dma_start(
                    out=xg[:, g % NX, :], out_offset=None, in_=io["x_norm"],
                    in_offset=bass.IndirectOffsetOnAxis(ap=rows_i[:, g:g + 1].bitcast(U32), axis=0)))

        def turn_rows(j):
            if j >= NT:
                pe.need(fetched[j], done["t_copy"].get(j - 2))
                for c in range(C):
                    ins = nc.tensor.transpose(bank(j % 2)[:, c * P:(c + 1) * P], xg[:, (j - NT) % NX, c * P:(c + 1) * P], ident[:])
                mark("t_turn", j, ins)

        def copy_rows(j):
            if j >= NT:
                act.need(done["t_turn"][j], done["t_gu"].get(j - 3))
                mark("t_copy", j, nc.scalar.copy(xgT[:, j % 3].rearrange("p c t -> p (c t)"), bank(j % 2)[:, 0:D]))

        def weights(j):
            if j < NT:
                pe.need(got_shared)
                return E
            pe.need(got_exp, expert_ready)
            return nc.tensor.value_load(expert_i[0:1, j - NT:j - NT + 1], min_val=0, max_val=E - 1)

        def gate_up(j, e):
            pe.need(done["t_clip"].get(j - 2), done["t_copy"].get(j) if j >= NT else x2T_ready[j])
            src = x2T[:, :, j * P:(j + 1) * P] if j < NT else xgT[:, j % 3]
            for c in range(C):
                w = W[:, bass.ds(e, 1), c * 2 * I:(c + 1) * 2 * I].rearrange("p o f -> p (o f)")
                ins = nc.tensor.matmul(bank(2 + j % 2)[:, 0:2 * I], src[:, c, :], w, start=(c == 0), stop=(c == C - 1))
            mark("t_gu", j, ins)

        def clip(j):
            dve.need(done["t_gu"][j], done["t_hid"].get(j - R), done["t_tanh"].get(j - R))
            mark("t_clip", j, nc.vector.tensor_scalar(gu[:, j % R, :], bank(2 + j % 2)[:, 0:2 * I], 7.0, -7.0, ALU.min, ALU.max))

        def tanh(j):
            act.need(done["t_clip"][j], done["t_gate"].get(j - R))
            mark("t_tanh", j, nc.scalar.activation(th[:, j % R, :], gu[:, j % R, 0:I], ACT.Tanh, scale=0.5))

        def hidden(j):
            q = j % R
            dve.need(done["t_tanh"][j], done["t_hturn"].get(j - R))
            mark("t_gate", j, nc.vector.scalar_tensor_tensor(out=hid[:, q, :], in0=th[:, q, :], scalar=1.0,
                                                             in1=gu[:, q, 0:I], op0=ALU.add, op1=ALU.mult))
            dve.need(done["t_gate"][j])
            mark("t_hid", j, nc.vector.tensor_tensor(hid[:, q, :], hid[:, q, :], gu[:, q, I:2 * I], ALU.mult))

        def turn_hidden(j):
            pe.need(done["t_hid"][j], done["t_hcopy"].get(j - 2))
            mark("t_hturn", j, nc.tensor.transpose(bank(4 + j % 2)[:, 0:P], hid[:, j % R, :], ident[:]))

        def copy_hidden(j):
            dve.need(done["t_hturn"][j], done["t_down"].get(j - R))
            mark("t_hcopy", j, nc.vector.tensor_copy(hidT[:, j % R, :], bank(4 + j % 2)[:, 0:P]))

        def down(j, e):
            pe.need(done["t_hcopy"][j], done["t_out"].get(j - 2))
            w = W[:, bass.ds(e, 1), 2 * C * I:FE].rearrange("p o f -> p (o f)")
            mark("t_down", j, nc.tensor.matmul(bank(6 + j % 2)[:, 0:D], hidT[:, j % R, :], w, start=True, stop=True))

        def finish(j):
            q = j % 2
            if j < NT:
                dve.need(done["t_down"][j])
                mark("t_out", j, nc.vector.scalar_tensor_tensor(out=x_sb[:, j, :], in0=bank(6 + q)[:, 0:D],
                                                                scalar=half_gate[:], in1=x_sb[:, j, :],
                                                                op0=ALU.mult, op1=ALU.add))
                return
            g = j - NT
            act.need(done["t_down"][j], stored.get(j - NY))
            mark("t_out", j, nc.scalar.copy(y_sb[:, g % NY, :], bank(6 + q)[:, 0:D]))
            sp.need(done["t_out"][j])
            stored[j] = st_y[g % NY].mark(nc.sync.dma_start(io["y_rows"][g * P:(g + 1) * P, :], y_sb[:, g % NY, :]))

        experts_of = {}
        for j in range(NT, NT + NX):
            fetch(j)
        LAG_C, LAG_G, LAG_H, LAG_T, LAG_D = 1, 2, 3, 5, 6
        for i in range(J + LAG_D):
            def due(lag):
                return i - lag if 0 <= i - lag < J else None
            j = due(0)
            if j is not None:
                turn_rows(j)
                copy_rows(j)
                if i + NX < J and i >= NT:
                    fetch(i + NX)
            j = due(LAG_T)
            if j is not None:
                turn_hidden(j)
                copy_hidden(j)
            j = due(LAG_G)
            if j is not None:
                gate_up(j, experts_of[j])
                clip(j)
                tanh(j)
            j = due(LAG_C)
            if j is not None:
                experts_of[j] = weights(j)
            j = due(LAG_H)
            if j is not None:
                hidden(j)
            j = due(LAG_D)
            if j is not None:
                down(j, experts_of.pop(j))
                finish(j)

        NG = 8
        yg = moved[:].rearrange("p n k e -> p (n k e)").rearrange("p (g d) -> p g d", g=NG)
        ld_yg = [stage(f"ld_yg{n}", 16) for n in range(NG)]
        s_acc = stage("s_acc")
        st_o = stage("st_o", 16)
        acc = []
        pool.need(y_ready, *(stored[j] for j in range(J - NY, J)))
        for m in range(NT * K):
            t, k = divmod(m, K)
            pool.need(acc[m - NG] if m >= NG else None)
            got = ld_yg[m % NG].mark(nc.gpsimd.indirect_dma_start(
                out=yg[:, m % NG, :], out_offset=None, in_=io["y_rows"],
                in_offset=bass.IndirectOffsetOnAxis(ap=y_i[:, m:m + 1].bitcast(U32), axis=0)))
            dve.need(got, acc[-1] if acc else None)
            acc.append(s_acc.mark(nc.vector.scalar_tensor_tensor(out=x_sb[:, t, :], in0=yg[:, m % NG, :],
                                                                 scalar=share[:, t, k:k + 1], in1=x_sb[:, t, :],
                                                                 op0=ALU.mult, op1=ALU.add)))
            if k == K - 1:
                sp.need(acc[-1])
                st_o.mark(nc.sync.dma_start(io["out"].rearrange("(n p) d -> n p d", p=P)[t], x_sb[:, t, :]))
        sp.need((st_o.sem, st_o.count))
        close_scope()


def kernel(x, ctx_2048, g_xattn, g_ffn, L0_xattn_Wq, L0_xattn_bq, L0_xattn_Wkv, L0_xattn_bkv, L0_xattn_Wp,
           L0_xattn_bp, L0_ffn_router_w, L0_ffn_expert_bias, L0_ffn_gate_w, L0_ffn_up_w, L0_ffn_down_w,
           L0_ffn_shared_gate_w, L0_ffn_shared_up_w, L0_ffn_shared_down_w):
    import concourse.bacc as bacc
    from concourse.bass_utils import run_bass_kernel_spmd as run

    n = np.asarray
    D = x.shape[-1]
    bkv = n(L0_xattn_bkv)
    gate = np.concatenate([n(L0_ffn_gate_w), n(L0_ffn_shared_gate_w)[None]])
    up = np.concatenate([n(L0_ffn_up_w), n(L0_ffn_shared_up_w)[None]])
    down = np.concatenate([n(L0_ffn_down_w), n(L0_ffn_shared_down_w)[None]])
    parts = []
    for c in range(D // 128):
        parts += [gate[:, :, c * 128:(c + 1) * 128].transpose(2, 0, 1), up[:, :, c * 128:(c + 1) * 128].transpose(2, 0, 1)]
    experts = np.concatenate(parts + [down.transpose(2, 0, 1)], axis=2).reshape(128, -1)
    arrays = {
        "x": n(x).reshape(-1, D),
        "ctxT": n(ctx_2048).reshape(-1, D).T,
        "wq": n(L0_xattn_Wq), "wkv": n(L0_xattn_Wkv), "wp": n(L0_xattn_Wp),
        "rows": np.concatenate([n(L0_xattn_bq), bkv[:D], n(L0_xattn_bp), n(g_xattn).reshape(1),
                                n(g_ffn).reshape(1)])[None, :],
        "bv": bkv[D:].reshape(-1, 128).T,
        "router_wT": n(L0_ffn_router_w).T,
        "expert_bias": n(L0_ffn_expert_bias)[None, :],
        "experts": experts,
    }
    arrays = {k: np.ascontiguousarray(a) for k, a in arrays.items()}
    nc = bacc.Bacc("TRN2", target_bir_lowering=False, num_devices=1)
    io = {k: nc.dram_tensor(f"in_{k}", a.shape, mybir.dt.from_np(a.dtype), kind="ExternalInput").ap()
          for k, a in arrays.items()}
    T = arrays["x"].shape[0]
    io["out"] = nc.dram_tensor("out_y", (T, D), F32, kind="ExternalOutput").ap()
    E, K = arrays["router_wT"].shape[1], 4
    io["slots"] = nc.dram_tensor("slots", (E * (T + 128), 1), F32, kind="Internal").ap()
    io["x_norm"] = nc.dram_tensor("x_norm", (T, D), F32, kind="Internal").ap()
    io["y_rows"] = nc.dram_tensor("y_rows", (((T * K - E) // 128 + E) * 128, D), F32, kind="Internal").ap()
    build(nc, io)
    r = run(nc, [{f"in_{k}": a for k, a in arrays.items()}], core_ids=[0])
    return r.results[0]["out_y"].reshape(x.shape)
```

```python
from contextlib import ExitStack

import numpy as np
import concourse.bass as bass
from concourse import mybir

ALU = mybir.AluOpType
ACT = mybir.ActivationFunctionType
AX = mybir.AxisListType
F32 = mybir.dt.float32
BF16 = mybir.dt.bfloat16
F16 = mybir.dt.float16
U8 = mybir.dt.uint8
U16 = mybir.dt.uint16
I32 = mybir.dt.int32
U32 = mybir.dt.uint32

P = 128
ROUND = 1.5 * 2.0 ** 23
OFFSET = 1024.0


class Stage:

    def __init__(self, sem, step=1):
        self.sem, self.step, self.count = sem, step, 0

    def mark(self, instruction):
        instruction.then_inc(self.sem, self.step)
        self.count += self.step
        return self.sem, self.count


class Engine:

    def __init__(self, eng):
        self.eng, self.seen = eng, {}

    def need(self, *steps):
        for step in steps:
            if step is None:
                continue
            sem, value = step
            if self.seen.get(id(sem), 0) < value:
                self.seen[id(sem)] = value
                self.eng.wait_ge(sem, value)
        return self.eng


def build(nc, io):
    T, D = io["x"].shape
    H, HD = 16, D // 16
    E, K = io["router_wT"].shape[1], 4
    I = io["experts"].shape[1] // (E + 1) // (3 * D // P)
    NT, C = T // P, D // P
    PAIRS = H // 2
    REGION = T + P
    NTILE = (T * K - E) // P + E
    BIG = float(2 ** 17)
    SENT = -3.0e38
    FE = 2 * C * I + D
    LN255 = float(np.log(np.float64(255.0)))

    with ExitStack() as ctx:
        scopes = [ctx]

        def sb(name, shape, dt=F32):
            return scopes[-1].enter_context(nc.sbuf_tensor(name, shape, dt))

        def open_scope():
            scopes.append(ExitStack())

        def close_scope():
            scopes.pop().close()

        def stage(name, step=1):
            return Stage(ctx.enter_context(nc.semaphore(name)), step)

        pe, dve, act, pool, sp = (Engine(e) for e in (nc.tensor, nc.vector, nc.scalar, nc.gpsimd, nc.sync))

        x_sb = sb("x_sb", [P, NT, D])
        xn = sb("xn", [P, NT, D])
        wp = sb("wp", [P, C, D])
        rows = sb("rows", [1, 3 * D + 2])
        bv = sb("bv", [P, C])
        wr = sb("wr", [P, C, E])
        eb = sb("eb", [1, E])
        bias_e = sb("bias_e", [P, E])
        x2T = sb("x2T", [P, C, T])
        before = sb("before", [P, P], BF16)
        ones_sq = sb("ones_sq", [P, P], BF16)
        region0 = sb("region0", [P, E])
        key0 = sb("key0", [P, E])
        iota_i = sb("iota_i", [P, E], I32)
        lane_i = sb("lane_i", [P, 1], I32)
        lane = sb("lane", [P, 1])
        token_i = sb("token_i", [P, NT], I32)
        token = sb("token", [P, NT])
        load = sb("load", [P, E], BF16)
        pos_i = sb("pos_i", [P, NT, K], I32)
        score_e = sb("score_e", [P, NT, E])
        keys = sb("keys", [P, NT, E])
        top_keys = sb("top_keys", [P, NT, 8])
        share = sb("share", [P, NT, K])
        ones = sb("ones", [1, P])
        ident = sb("ident", [P, P])
        ident_b = sb("ident_b", [P, P], BF16)
        gates = sb("gates", [P, 2])
        banks = ctx.enter_context(nc.psum_tensor("banks", [P, 8, 512], F32))

        open_scope()
        arena = sb("arena", [P, (NT * H * P + PAIRS * T + NT * D) // 2])
        Q_END, K_END = NT * H * P, NT * H * P + PAIRS * T
        arena_b = arena[:].bitcast(BF16)
        qT = arena_b[:, 0:Q_END].rearrange("p (t h q) -> p t h q", t=NT, h=H)
        kT = arena_b[:, Q_END:K_END].rearrange("p (c t) -> p c t", c=PAIRS)
        v_int = arena_b[:, K_END:K_END + NT * D].rearrange("p (n d) -> p n d", n=NT)
        W = arena[:, 0:(E + 1) * FE].rearrange("p (e f) -> p e f", e=E + 1)
        v_corr = sb("v_corr", [P, NT // 2, D], F16)
        minus_offset = sb("minus_offset", [P, P], F16)
        sq = sb("sq", [P, NT, H])
        neg_sq = sb("neg_sq", [P, NT, H])
        open_scope()
        wq = sb("wq", [P, C, D])
        wkv = sb("wkv", [P, C, 2 * D])
        xT = sb("xT", [P, C, T])
        cT = x2T
        vT = xn[:].rearrange("p n d -> p (n d)").rearrange("p (c t) -> p c t", c=C)

        ld_x = stage("ld_x", 16)
        ld_w = stage("ld_w", 16)
        ld_c = stage("ld_c", 16)
        ld_l = stage("ld_l", 16)
        got_x = ld_x.mark(nc.sync.dma_start(x_sb[:], io["x"].rearrange("(n p) d -> p n d", p=P)))
        for src, dst in ((io["wq"], wq), (io["wkv"], wkv)):
            got_w = ld_w.mark(nc.sync.dma_start(dst[:], src.rearrange("(c p) d -> p c d", p=P)))
        got_w = ld_w.mark(nc.sync.dma_start(rows[:], io["rows"]))
        got_w = ld_w.mark(nc.sync.dma_start(bv[:], io["bv"]))
        got_c = ld_c.mark(nc.scalar.dma_start(cT[:], io["ctxT"].rearrange("(c p) t -> p c t", p=P)))
        got_l = ld_l.mark(nc.scalar.dma_start(wp[:], io["wp"].rearrange("(c p) d -> p c d", p=P)))
        got_l = ld_l.mark(nc.scalar.dma_start(wr[:], io["router_wT"].rearrange("(c p) e -> p c e", p=P)))
        got_l = ld_l.mark(nc.scalar.dma_start(eb[:], io["expert_bias"]))

        consts = stage("consts")
        made = consts.mark(nc.gpsimd.memset(ident[:], 0.0))
        pool.need(made)
        made = consts.mark(nc.gpsimd.affine_select(out=ident[:], in_=ident[:], compare_op=ALU.not_equal, fill=1.0,
                                                   base=0, pattern=[[-1, P]], channel_multiplier=1))
        pool.need(made)
        consts.mark(nc.gpsimd.tensor_copy(ident_b[:], ident[:]))
        got_const = consts.mark(nc.gpsimd.memset(ones[:], 1.0))
        consts.mark(nc.gpsimd.memset(ones_sq[:], 1.0))
        consts.mark(nc.gpsimd.memset(load[:], 0.0))
        consts.mark(nc.gpsimd.iota(iota_i[:], pattern=[[REGION, E]], base=0, channel_multiplier=0))
        consts.mark(nc.gpsimd.iota(lane_i[:], pattern=[[0, 1]], base=0, channel_multiplier=1))
        consts.mark(nc.gpsimd.iota(token_i[:], pattern=[[P, NT]], base=0, channel_multiplier=1))
        pool.need((consts.sem, consts.count))
        consts.mark(nc.gpsimd.tensor_copy(token[:], token_i[:]))
        consts.mark(nc.gpsimd.tensor_copy(region0[:], iota_i[:]))
        consts.mark(nc.gpsimd.tensor_copy(lane[:], lane_i[:]))
        pool.need((consts.sem, consts.count))
        consts.mark(nc.gpsimd.tensor_scalar(key0[:], region0[:], -1.0, BIG, ALU.mult, ALU.add))
        consts.mark(nc.gpsimd.affine_select(out=before[:], in_=ones_sq[:], compare_op=ALU.is_gt, fill=0.0,
                                            base=0, pattern=[[1, P]], channel_multiplier=-1))
        zeroed = consts.mark(nc.gpsimd.memset(arena_b[:, 0:Q_END], 0.0))
        consts.mark(nc.gpsimd.memset(v_corr[:], 0.0))
        consts_all = consts.mark(nc.gpsimd.memset(minus_offset[:], -OFFSET))

        st_e = stage("st_e", 16)
        sp.need(consts_all)
        slots_clear = st_e.mark(nc.sync.dma_start(io["slots"].rearrange("(p n) o -> p (n o)", p=P),
                                                      v_corr[:].rearrange("p n d -> p (n d)").bitcast(F32)[:, 0:E * REGION // P]))

        chain = stage("chain")

        def then(instruction):
            dve.need(chain.mark(instruction))

        root_s = stage("root_s")

        def first_inverse_root(out, var, tmp, y):
            then(nc.vector.tensor_scalar(tmp, var, 1e-5, None, ALU.add))
            act.need((chain.sem, chain.count))
            got = root_s.mark(nc.scalar.activation(y, tmp, ACT.Sqrt))
            dve.need(got)
            then(nc.vector.reciprocal(out, y))
            then(nc.vector.tensor_tensor(out, out, tmp, ALU.mult))
            then(nc.vector.tensor_tensor(out, out, y, ALU.add))
            then(nc.vector.tensor_scalar(out, out, 0.5, None, ALU.mult))
            then(nc.vector.reciprocal(out, out))

        stats = sb("stats", [P, NT, 6])
        mv = sb("mv", [P, NT, 2])
        rstd = sb("rstd", [P, NT])
        root_t = sb("root_t", [P, NT])
        root_y = sb("root_y", [P, NT])
        normed = stage("normed")

        def layer_norm():
            for n in range(NT):
                ins = nc.vector.bn_stats(stats[:, n, :], x_sb[:, n, :])
            then(ins)
            for n in range(NT):
                ins = nc.vector.bn_aggr(mv[:, n, :], stats[:, n, :])
            then(ins)
            first_inverse_root(rstd[:], mv[:, :, 1], root_t[:], root_y[:])
            steps = []
            for n in range(NT):
                steps.append(normed.mark(nc.vector.tensor_scalar(xn[:, n, :], x_sb[:, n, :], mv[:, n, 0:1],
                                                                 rstd[:, n:n + 1], ALU.subtract, ALU.mult)))
            return steps

        turned = stage("turned")
        turned_out = stage("turned_out")
        free = {}

        def bank(k):
            return banks[:, k, :]

        def turn(src, dst, ready):
            out = []
            for g in range(NT // 2):
                k = g % 2
                pe.need(got_const, ready[2 * g], ready[2 * g + 1], free.get(k))
                for c in range(C):
                    for n in range(2):
                        ins = nc.tensor.transpose(bank(k)[:, (2 * c + n) * P:(2 * c + n + 1) * P],
                                                  src[:, 2 * g + n, c * P:(c + 1) * P], ident[:])
                got = turned.mark(ins)
                act.need(got)
                step = turned_out.mark(nc.scalar.copy(dst[:, :, 2 * g * P:(2 * g + 2) * P],
                                                      bank(k).rearrange("p (c t) -> p c t", c=C)))
                free[k] = step
                out.append(step)
            return out

        s_gate = stage("s_gate")
        pe.need(got_const, got_w, got_l)
        nc.tensor.matmul(bank(6)[:, 0:2], ones[:], rows[:, 3 * D:3 * D + 2], start=True, stop=True)
        ins = nc.tensor.matmul(bank(6)[:, 2:2 + E], ones[:], eb[:], start=True, stop=True)
        act.need(s_gate.mark(ins))
        s_gate.mark(nc.scalar.copy(bias_e[:], bank(6)[:, 2:2 + E]))
        gate_step = s_gate.mark(nc.scalar.activation(gates[:], bank(6)[:, 0:2], ACT.Tanh))
        free[6] = gate_step

        proj = stage("proj")
        q4 = sb("q4", [P, 2, 2, H, 4, HD], BF16)
        quant0 = sb("quant0", [P, 2, H, HD])
        kfull0 = sb("kfull0", [P, 2, H, HD])
        quant = [quant0[:], keys[:].rearrange("p n e -> p (n e)").rearrange("p (n h d) -> p n h d", n=2, h=H)]
        kfull = [kfull0[:], score_e[:].rearrange("p n e -> p (n e)").rearrange("p (n h d) -> p n h d", n=2, h=H)]
        amax = sb("amax", [P, 2, H])
        rec = sb("rec", [P, 2, H])
        sk = sb("sk", [P, 2, 2, H])
        then(nc.vector.memset(q4[:], 0.0))
        in_setup = {"dve": chain, "pool": stage("setup_pool"), "act": stage("setup_act")}
        turn4 = stage("turn4")
        sums_s = stage("sums_s")
        items = [("k", g) for g in range(NT // 2)] + [("q", g) for g in range(NT // 2)]
        q4_read, cut_done, projected = {}, {}, {}
        SLOT_BANKS = 4

        def did(name, instruction):
            return in_setup[name].mark(instruction)

        def project(n):
            what, g = items[n]
            k = (n + 2) % SLOT_BANKS
            row, w, src, src_step = (1, wkv, cT, got_c) if what == "k" else (0, wq, xT, xT_steps[g])
            pe.need(src_step, got_w, got_const, free.get(k))
            for m in range(2):
                o = bank(k)[:, m * D:(m + 1) * D]
                for c in range(C):
                    nc.tensor.matmul(o, src[:, c, (2 * g + m) * P:(2 * g + m + 1) * P], w[:, c, 0:D], start=(c == 0), stop=False)
                ins = nc.tensor.matmul(o, ones[:], rows[:, row * D:(row + 1) * D], start=False, stop=True)
            projected[n] = proj.mark(ins)

        def quantise(n):
            what, g = items[n]
            k, b = (n + 2) % SLOT_BANKS, n % 2
            x = quant[b]
            ps = bank(k).rearrange("p (n h d) -> p n h d", n=2, h=H)
            s = sk[:, b] if what == "k" else sq[:, 2 * g:2 * g + 2, :]
            scale = 1.0 if what == "k" else 0.25
            dve.need(projected[n], cut_done.get(n - 2))
            then(nc.vector.tensor_reduce(amax[:], ps, AX.X, ALU.max, apply_absolute_value=True))
            then(nc.vector.tensor_scalar(s, amax[:], scale / 127.0, 1e-8, ALU.mult, ALU.max))
            then(nc.vector.reciprocal(rec[:], s))
            if scale != 1.0:
                then(nc.vector.tensor_scalar(rec[:], rec[:], scale, None, ALU.mult))
            free[k] = a = did("dve", nc.vector.tensor_tensor(x, ps, rec[:].unsqueeze(3).broadcast_to([P, 2, H, HD]), ALU.mult))
            dve.need(a)
            then(nc.vector.tensor_scalar(x, x, 127.0, -127.0, ALU.min, ALU.max))
            if what == "q":
                dve.need(q4_read.get(n - 2))
                x = q4[:, b, :, :, 0, :]
            whole[n] = did("dve", nc.vector.tensor_scalar(x, quant[b], ROUND, ROUND, ALU.add, ALU.subtract))

        def fill_slots(n):
            what, g = items[n]
            b = n % 2
            x = quant[b]
            hi, mid, lo = (q4[:, b, :, :, j, :] for j in range(3))
            if what == "q":
                pool.need(whole[n])
                did("pool", nc.gpsimd.tensor_copy(mid, hi))
                cut_done[n] = did("pool", nc.gpsimd.tensor_copy(lo, hi))
                return
            pool.need(whole[n])
            a = did("pool", nc.gpsimd.tensor_tensor(kfull[b], x, sk[:, b].unsqueeze(3).broadcast_to([P, 2, H, HD]), ALU.mult))
            act.need(a, q4_read.get(n - 2))
            a = did("act", nc.scalar.copy(hi, kfull[b]))
            pool.need(a)
            a = did("pool", nc.gpsimd.tensor_tensor(x, kfull[b], hi, ALU.subtract))
            act.need(a)
            a = did("act", nc.scalar.copy(mid, x))
            pool.need(a)
            cut_done[n] = did("pool", nc.gpsimd.tensor_tensor(lo, x, mid, ALU.subtract))

        whole = {}

        def turn_item(n):
            what, g = items[n]
            b = n % 2
            for m in range(2):
                k2 = 4 + m
                t0 = (2 * g + m) * P
                pe.need(cut_done[n], *free.get(k2, ()))
                tb = bank(k2).bitcast(BF16)
                for pair in range(PAIRS):
                    ins = nc.tensor.transpose(tb[:, pair * P:(pair + 1) * P],
                                              q4[:, b, m, 2 * pair:2 * pair + 2, :, :].rearrange("p h s d -> p (h s d)"),
                                              ident_b[:])
                a = turn4.mark(ins)
                q4_read[n] = a
                act.need(a)
                tb = tb.rearrange("p (c t) -> p c t", c=PAIRS)
                if what == "k":
                    free[k2] = (did("act", nc.scalar.copy(kT[:, :, t0:t0 + P], tb)),)
                elif m == 0:
                    act.need(*zeroed_all)
                    did("act", nc.scalar.copy(qT[0:64, 2 * g + m, 0:H:2, :], tb[0:64]))
                    free[k2] = (did("act", nc.scalar.copy(qT[64:P, 2 * g + m, 1:H:2, :], tb[64:P])),)
                else:
                    act.need(*zeroed_all)
                    x1 = did("act", nc.scalar.copy(qT[0:64, 2 * g + m, 0:H:2, :], tb[0:64]))
                    dve.need(a, *zeroed_all)
                    free[k2] = (x1, did("dve", nc.vector.tensor_copy(qT[64:P, 2 * g + m, 1:H:2, :], tb[64:P])))

        vproj = stage("vproj")
        vout = stage("vout")
        vmax = sb("vmax", [P, C])
        sv = sb("sv", [P, C])
        rv = sb("rv", [P, C])
        vTi = qT[:, NT - 2:NT].rearrange("p t h q -> p t (h q)")
        ones_b = sb("ones_b", [P, 2], BF16)

        def project_v():
            for c in range(C):
                for t in range(T // 512):
                    k = 6 + t % 2
                    pe.need(free.get(k), got_w, got_c)
                    for d in range(C):
                        ins = nc.tensor.matmul(bank(k), wkv[:, d, D + c * P:D + (c + 1) * P],
                                               cT[:, d, t * 512:(t + 1) * 512], start=(d == 0), stop=(d == C - 1))
                    act.need(vproj.mark(ins), (turned.sem, turned.count))
                    free[k] = vout.mark(nc.scalar.activation(vT[:, c, t * 512:(t + 1) * 512], bank(k), ACT.Identity,
                                                             bias=bv[:, c:c + 1]))

        def quantise_v():
            dve.need((vout.sem, vout.count))
            then(nc.vector.tensor_reduce(vmax[:], vT, AX.X, ALU.max, apply_absolute_value=True))
            then(nc.vector.tensor_scalar(sv[:], vmax[:], 1.0 / 127.0, 1e-8, ALU.mult, ALU.max))
            then(nc.vector.reciprocal(rv[:], sv[:]))
            for c in range(C):
                ins = nc.vector.tensor_scalar(vT[:, c, :], vT[:, c, :], rv[:, c:c + 1], 127.0, ALU.mult, ALU.min)
            then(ins)
            then(nc.vector.tensor_scalar(vT, vT, -127.0, ROUND, ALU.max, ALU.add))
            dve.need(zeroed)
            then(nc.vector.tensor_scalar(vTi, vT, ROUND, None, ALU.subtract))

        def turn_v(g):
            k = 6 + g % 2
            pe.need(v_round, free.get(k))
            tb = bank(k).bitcast(BF16)
            for n in range(4):
                for c in range(C):
                    ins = nc.tensor.transpose(tb[:, (2 * n + c) * P:(2 * n + c + 1) * P],
                                              vTi[:, c, (4 * g + n) * P:(4 * g + n + 1) * P], ident_b[:])
            act.need(turn4.mark(ins))
            free[k] = did("act", nc.scalar.copy(v_int[:, 4 * g:4 * g + 4, :], tb.rearrange("p (n d) -> p n d", n=4)))

        vs_hi = vT[0:2, 0, 0:D].bitcast(F16)
        vs_lo = vT[0:2, 1, 0:2 * D]

        def sum_v(g):
            k = 6 + g % 2
            pe.need(free.get(k))
            for n in range(4):
                ins = nc.tensor.matmul(bank(k)[0:2, (n // 2) * D:(n // 2 + 1) * D], ones_b[:], v_int[:, 4 * g + n, :],
                                       start=(n % 2 == 0), stop=(n % 2 == 1))
            dve.need(sums_s.mark(ins))
            sums = bank(k)[0:2, :]
            then(nc.vector.tensor_copy(vs_hi, sums))
            then(nc.vector.tensor_tensor(vs_lo, sums, vs_hi, ALU.subtract))
            free[k] = (chain.sem, chain.count)
            then(nc.vector.tensor_scalar(vs_lo, vs_lo, ident[0:2, 1:2], None, ALU.mult))
            then(nc.vector.scalar_tensor_tensor(out=v_corr[0:2, 2 * g:2 * g + 2, :].rearrange("p n d -> p (n d)"),
                                                in0=vs_hi, scalar=ident[0:2, 0:1], in1=vs_lo,
                                                op0=ALU.mult, op1=ALU.add))

        zeroed_all = [zeroed]
        then(nc.vector.memset(ones_b[:], 1.0))
        for n in range(2):
            project(n)
        dve.need(got_x)
        steps = layer_norm()
        xT_steps = turn(xn, xT, steps)
        project_v()
        dve.need(got_l)
        for n in range(len(items)):
            if n + 2 < len(items):
                project(n + 2)
            quantise(n)
            if n == 1:
                quantise_v()
                v_round = (chain.sem, chain.count)
                for c in range(C):
                    ins = nc.vector.tensor_scalar(wp[:, c, :], wp[:, c, :], sv[:, c:c + 1], None, ALU.mult)
                then(ins)
                wp_scaled = (chain.sem, chain.count)
            if 2 <= n < 2 + NT // 4:
                turn_v(n - 2)
                if n == 1 + NT // 4:
                    pool.need((turn4.sem, turn4.count))
                    zeroed_all.append(did("pool", nc.gpsimd.memset(vTi, 0.0)))
                    pe.need((in_setup["act"].sem, in_setup["act"].count))
                    dve.need(got_const, consts_all, slots_clear)
            if 2 + NT // 4 <= n < 2 + NT // 2:
                sum_v(n - 2 - NT // 4)
            if n > 0:
                turn_item(n - 1)
            fill_slots(n)
        turn_item(len(items) - 1)
        then(nc.vector.tensor_scalar(neg_sq[:], sq[:], -1.0, None, ALU.mult))
        setup_over = [(in_setup[e].sem, in_setup[e].count) for e in ("dve", "pool", "act")]
        k_ready = q_ready = v_ready = setup_over[2]
        v_ready2 = setup_over[0]

        close_scope()
        NB = 4
        NW = 3
        words = sb("words", [P, NW, T], U16)
        pT = sb("pT", [P, NB, NT, P], F16)
        MR = 8
        hmax = sb("hmax", [P, MR, 4])
        umax = sb("umax", [P, MR])
        nb_t = sb("nb_t", [P, MR])
        nbias = sb("nbias", [P, MR])
        psums = sb("psums", [P, NT, H, 2])
        norm = sb("norm", [P, NT, H])
        pool.need(*setup_over)
        filled = consts.mark(nc.gpsimd.memset(words[:], 0x6400))
        free.clear()
        heads_out = xn

        s_mm, s_max, s_two, s_neg, s_bias, s_exp = (stage(n) for n in ("s_mm", "s_max", "s_two", "s_neg", "s_bias", "s_exp"))
        s_sc, s_pv = stage("s_sc"), stage("s_pv")
        s_turn = [stage(f"s_turn{n}", 16) for n in range(NB)]
        U = NT * H
        scored, maxd, scored2, expd, turnd, pvd, biasd, normd = ({} for _ in range(8))
        bytes_of = words[:].bitcast(U8).rearrange("p b (t two) -> p b t two", two=2)
        word_f16 = words[:].bitcast(F16)

        def score(out, u, k0):
            t, h = divmod(u, H)
            return nc.tensor.matmul(out, qT[:, t, h, :], kT[:, h // 2, k0:k0 + 512], start=True, stop=True)

        def do_scores_max(u, m):
            j = 4 * u + m
            pe.need(*setup_over, maxd.get(j - 2), free.get(j % 2))
            scored[j] = s_mm.mark(score(bank(j % 2), u, m * 512))

        def do_max(u, m):
            j = 4 * u + m
            dve.need(scored[j], biasd.get(u - MR))
            maxd[j] = s_max.mark(nc.vector.tensor_reduce(hmax[:, u % MR, m:m + 1], bank(j % 2), AX.X, ALU.max))

        def do_bias(u):
            t, h = divmod(u, H)
            r = u % MR
            two = slice(r, r + 2)
            dve.need(maxd[4 * u + 7], biasd.get(u - MR))
            pool.need(s_two.mark(nc.vector.tensor_reduce(umax[:, two], hmax[:, two, :], AX.X, ALU.max)))
            pool.need(expd.get(2 * (u + 1 - MR) + 1), q_ready)
            pool.need(s_neg.mark(nc.gpsimd.tensor_tensor(nb_t[:, two], umax[:, two], neg_sq[:, t, h:h + 2], ALU.mult)))
            biasd[u] = biasd[u + 1] = s_bias.mark(nc.gpsimd.tensor_scalar(nbias[:, two], nb_t[:, two], LN255, None, ALU.add))

        def do_scores_exp(u, half):
            j = 2 * u + half
            pe.need(expd.get(j - 2), free.get(3 + 2 * (j % 2)), free.get(4 + 2 * (j % 2)))
            for m in range(2):
                ins = score(bank(3 + 2 * (j % 2) + m), u, (2 * half + m) * 512)
            scored2[j] = s_sc.mark(ins)

        def do_exp(u, half):
            t, h = divmod(u, H)
            j = 2 * u + half
            b0 = 3 + 2 * (j % 2)
            act.need(scored2[j], biasd[u], filled, turnd.get(u - NW))
            expd[j] = s_exp.mark(nc.scalar.activation(
                bytes_of[:, u % NW, half * (T // 2):(half + 1) * (T // 2), 0:1],
                banks[:, b0:b0 + 2, :].rearrange("p m (n o) -> p (m n) o", o=1), ACT.Exp,
                bias=nbias[:, u % MR:u % MR + 1], scale=sq[:, t, h:h + 1], accum_out=psums[:, t, h, half:half + 1]))

        def do_turn(u):
            sp.need(expd[2 * u + 1], pvd.get(u - NB))
            turnd[u] = s_turn[u % NB].mark(nc.sync.dma_start_transpose(pT[:, u % NB, :, :], word_f16[:, u % NW, :]))

        def do_pv(u, half):
            t, h = divmod(u, H)
            cols = slice(h * HD, (h + 1) * HD)
            pe.need(turnd[u], v_ready, v_ready2, normd.get(t - 1))
            for kt in range(half * NT // 2, (half + 1) * NT // 2):
                ins = nc.tensor.matmul(bank(7)[:, cols], pT[:, u % NB, kt, :], v_int[:, kt, cols],
                                       start=(kt == 0), stop=(kt == NT - 1))
                if kt % 2 == 0:
                    nc.tensor.matmul(bank(7)[:, cols], minus_offset[:], v_corr[:, kt // 2, cols], start=False, stop=False)
            step = s_pv.mark(ins)
            if half == 1:
                pvd[u] = step

        by = {name: stage(f"by_{name}") for name in ("pe", "dve", "act", "pool")}
        queue = {"pe": pe, "dve": dve, "act": act, "pool": pool}

        def does(name, instruction):
            return by[name].mark(instruction)

        hT_t = sb("hT_t", [P, C, P])
        stat = sb("stat", [P, 6])
        mean_var = sb("mean_var", [P, 2])
        small = sb("small", [P, 8])
        logit = sb("logit", [P, E])
        relu = sb("relu", [P, E])
        w1, w2, w3, w4 = (sb(f"w{n}", [P, E]) for n in range(1, 5))
        choose = sb("choose", [P, E + 8])
        chosen = sb("chosen", [P, E + 8])
        top = sb("top", [P, 8])
        top4 = sb("top4", [P, 8])
        mask_b = sb("mask_b", [P, E], BF16)
        consts.mark(nc.gpsimd.memset(choose[:], SENT))
        fillers = consts.mark(nc.gpsimd.memset(top4[:], SENT))
        st_x = stage("st_x", 16)
        st_xn = stage("st_xn", 16)
        post_bank = bank(2)
        half_a, half_b = post_bank[:, 0:D], post_bank[:, D:2 * D]

        def do_norm_scale(t):
            n = norm[:, t, :]
            pool.need(expd[2 * (t * H + H - 1) + 1])
            dve.need(does("pool", nc.gpsimd.tensor_tensor(n, psums[:, t, :, 0], psums[:, t, :, 1], ALU.add)))
            pool.need(does("dve", nc.vector.reciprocal(n, n)))
            normd[t] = does("pool", nc.gpsimd.tensor_scalar(n, n, 1e-8, None, ALU.max))

        def do_norm(t):
            dve.need(normd[t], pvd[t * H + H - 1])
            normd[t] = does("dve", nc.vector.tensor_tensor(
                heads_out[:, t, :].rearrange("p (h d) -> p h d", h=H), bank(7)[:, 0:D].rearrange("p (h d) -> p h d", h=H),
                norm[:, t, :].unsqueeze(2).broadcast_to([P, H, HD]), ALU.mult))

        def later(steps):
            for _ in range(steps):
                yield

        def helper(t):
            if t < NT - 1:
                return "pool", nc.gpsimd
            dve.need(by_now("pool"))
            return "dve", nc.vector

        def ops(eng, *instructions):
            for make in instructions:
                step = does(eng, make())
                queue[eng].need(step)
            return step

        def inverse_root(t, x, y, t1, x_step):
            eng, alu = helper(t)
            dve.need(x_step)
            a = does("dve", nc.vector.tensor_scalar(y.bitcast(I32), x.bitcast(I32), 1, None, ALU.arith_shift_right))
            yield
            queue[eng].need(a)
            ops(eng, lambda: alu.tensor_scalar(y.bitcast(I32), y.bitcast(I32), -1.0, float(0x5f3759df),
                                                     ALU.mult, ALU.add))
            yield
            for _ in range(3):
                ops(eng, lambda: alu.tensor_tensor(t1, y, y, ALU.mult),
                         lambda: alu.tensor_tensor(t1, t1, x, ALU.mult))
                yield
                a = ops(eng, lambda: alu.tensor_scalar(t1, t1, -0.5, 1.5, ALU.mult, ALU.add),
                             lambda: alu.tensor_tensor(y, y, t1, ALU.mult))
                yield
            return a

        bank2 = {"written": None, "read": free.get(2)}

        def write_bank2(*instructions, last=True):
            pe.need(bank2["read"])
            for make in instructions:
                ins = make()
            bank2["written"] = does("pe", ins)
            return bank2["written"]

        def read_bank2(name, make):
            queue[name].need(bank2["written"])
            bank2["read"] = does(name, make())
            return bank2["read"]

        def close_layer(t):
            eng, alu = helper(t)
            xt = x_sb[:, t, :]
            ts = slice(t * P, (t + 1) * P)
            yield from later(2)
            pe.need(normd[t])
            write_bank2(*(lambda c=c: nc.tensor.transpose(half_a[:, c * P:(c + 1) * P], heads_out[:, t, c * P:(c + 1) * P],
                                                          ident[:]) for c in range(C)))
            yield
            a = read_bank2("act", lambda: nc.scalar.copy(hT_t[:].rearrange("p c t -> p (c t)"), half_a))
            yield from later(3)
            pe.need(a, wp_scaled)
            for c in range(C):
                write_bank2(lambda: nc.tensor.matmul(half_a, hT_t[:, c, :], wp[:, c, :], start=(c == 0), stop=False))
                projecting[0] = True
                yield
            write_bank2(lambda: nc.tensor.matmul(half_a, ones[:], rows[:, 2 * D:3 * D], start=False, stop=True))
            projecting[0] = False
            yield
            dve.need(gate_step)
            a = read_bank2("dve", lambda: nc.vector.scalar_tensor_tensor(out=xt, in0=half_a, scalar=gates[:, 0:1],
                                                                         in1=xt, op0=ALU.mult, op1=ALU.add))
            yield
            dve.need(a)
            a = does("dve", nc.vector.bn_stats(stat[:], xt))
            yield
            dve.need(a)
            a = does("dve", nc.vector.bn_aggr(mean_var[:], stat[:]))
            yield
            v, r, t1 = small[:, 0:1], small[:, 1:2], small[:, 2:3]
            queue[eng].need(a)
            a = ops(eng, lambda: alu.tensor_scalar(v, mean_var[:, 1:2], 1e-5, None, ALU.add))
            yield from later(2)
            a = yield from inverse_root(t, v, r, t1, a)
            yield from later(3)
            dve.need(a)
            a = does("dve", nc.vector.tensor_scalar(xn[:, t, :], xt, mean_var[:, 0:1], r, ALU.subtract, ALU.mult))
            sp.need(a)
            st_xn.mark(nc.sync.dma_start(io["x_norm"][t * P:(t + 1) * P, :], xn[:, t, :]))
            yield from later(3)
            pe.need(a)
            write_bank2(*(lambda c=c: nc.tensor.transpose(half_a[:, c * P:(c + 1) * P], xn[:, t, c * P:(c + 1) * P],
                                                          ident[:]) for c in range(C)))
            yield
            a = x2T_ready[t] = read_bank2("act", lambda: nc.scalar.copy(
                x2T[:, :, ts], half_a.rearrange("p (c t) -> p c t", c=C)))
            yield from later(3)
            pe.need(a)
            write_bank2(*(lambda c=c: nc.tensor.matmul(half_a[:, 0:E], x2T[:, c, ts], wr[:, c, :], start=(c == 0),
                                                       stop=(c == C - 1)) for c in range(C)))
            yield
            dve.need(logit_read[0])
            logit_ready[t] = read_bank2("dve", lambda: nc.vector.tensor_copy(logit[:], half_a[:, 0:E]))
            yield

        def choose_experts(t):
            eng, alu = helper(t)
            dve.need(logit_ready[t])
            a = does("dve", nc.vector.scalar_tensor_tensor(out=w1[:], in0=logit[:], scalar=-1.0, in1=logit[:],
                                                           op0=ALU.mult, op1=ALU.min))
            queue[eng].need(logit_ready[t])
            positive = logit_read[0] = ops(eng, lambda: alu.tensor_scalar(relu[:], logit[:], 0.0, None, ALU.max))
            yield from later(2)
            act.need(a)
            a = does("act", nc.scalar.activation(w2[:], w1[:], ACT.Exp))
            yield from later(3)
            queue[eng].need(a)
            a = ops(eng, lambda: alu.tensor_scalar(w3[:], w2[:], 2.0, None, ALU.add))
            yield from later(2)
            dve.need(a)
            a = does("dve", nc.vector.reciprocal(w3[:], w3[:]))
            yield
            queue[eng].need(a)
            ops(eng, lambda: alu.tensor_tensor(w3[:], w3[:], w2[:], ALU.mult),
                     lambda: alu.tensor_tensor(w4[:], w3[:], w3[:], ALU.mult))
            yield
            ops(eng, lambda: alu.tensor_scalar(w1[:], w4[:], 1 / 15, 1 / 13, ALU.mult, ALU.add))
            for m in (11, 9, 7, 5, 3, 1):
                ops(eng, lambda: alu.tensor_tensor(w1[:], w1[:], w4[:], ALU.mult),
                         lambda: alu.tensor_scalar(w1[:], w1[:], 1 / m, None, ALU.add))
                yield
            ops(eng, lambda: alu.tensor_tensor(w1[:], w1[:], w3[:], ALU.mult),
                     lambda: alu.tensor_scalar(w1[:], w1[:], 2.0, None, ALU.mult))
            yield
            a = ops(eng, lambda: alu.tensor_tensor(w1[:], w1[:], relu[:], ALU.add))
            yield from later(3)
            a = yield from inverse_root(t, w1[:], w2[:], w4[:], a)
            queue[eng].need(fillers, gate_step)
            a = ops(eng, lambda: alu.tensor_tensor(score_e[:, t, :], w2[:], w1[:], ALU.mult),
                         lambda: alu.tensor_tensor(choose[:, 0:E], score_e[:, t, :], bias_e[:], ALU.add))
            yield from later(3)
            dve.need(a)
            a = does("dve", nc.vector.max(top[:], choose[:]))
            yield
            queue[eng].need(a)
            a = ops(eng, lambda: alu.tensor_copy(top4[:, 0:K], top[:, 0:K]))
            yield from later(2)
            dve.need(a)
            a = does("dve", nc.vector.match_replace(chosen[:], top4[:], choose[:], SENT))
            yield
            queue[eng].need(a)
            a = ops(eng, lambda: alu.tensor_scalar(mask_b[:], chosen[:, 0:E], SENT, None, ALU.is_equal))
            yield from later(4)
            while projecting[0]:
                yield
            pe.need(a)
            ranked = write_bank2(lambda: nc.tensor.matmul(half_b[:, 0:E], before[:], mask_b[:], start=True, stop=False),
                                 lambda: nc.tensor.matmul(half_b[:, 0:E], ones_sq[:], load[:], start=False, stop=True))
            a = read_bank2("dve", lambda: nc.vector.scalar_tensor_tensor(
                out=keys[:, t, :], in0=half_b[:, 0:E], scalar=-1.0, in1=key0[:], op0=ALU.mult, op1=ALU.add))
            yield
            queue[eng].need(a, ranked)
            a = does(eng, alu.tensor_tensor(keys[:, t, :], keys[:, t, :], mask_b[:], ALU.mult))
            does(eng, alu.tensor_tensor(load[:], load[:], mask_b[:], ALU.add))
            yield from later(2)
            dve.need(a)
            a = does("dve", nc.vector.max(top_keys[:, t, :], keys[:, t, :]))
            yield
            queue[eng].need(a)
            a = ops(eng, lambda: alu.tensor_scalar(pos_i[:, t, :], top_keys[:, t, 0:K], -1.0, BIG, ALU.mult, ALU.add))
            yield
            pool.need(a, slots_clear)
            for k in range(K):
                st_x.mark(nc.gpsimd.indirect_dma_start(
                    out=io["slots"], out_offset=bass.IndirectOffsetOnAxis(ap=pos_i[:, t, k:k + 1].bitcast(U32), axis=0),
                    in_=token[:, t:t + 1], in_offset=None))
                yield from later(2)

        projecting, logit_read, logit_ready = [False], [None], {}

        def by_now(name):
            return by[name].sem, by[name].count

        x2T_ready = {}

        to_close, to_route = [], []

        def advance():
            if to_close and next(to_close[0][1], "over") == "over":
                t, _ = to_close.pop(0)
                to_route.append(choose_experts(t))
            if to_route and next(to_route[0], "over") == "over":
                to_route.pop(0)

        ld_w2 = [stage(f"ld_w2_{n}", 16) for n in range(2)]
        slots_got, slots_asked = [], [0]

        def load_weights(tiles_over, steps):
            n = slots_asked[0]
            if n <= E and (n + 1) * FE * 4 <= tiles_over * H * P * 2:
                ask_weights(steps)

        def ask_weights(steps):
            n = slots_asked[0]
            sp.need(*steps)
            slots_got.append(ld_w2[n % 2].mark(nc.sync.dma_start(W[:, n, :], io["experts"][:, n * FE:(n + 1) * FE])))
            slots_asked[0] += 1

        LAG_X, LAG_V = 3, 6
        for i in range(U + LAG_V):
            a, v = i - LAG_X, i - LAG_V
            for half in range(2):
                if i < U:
                    do_scores_max(i, 2 * half)
                    do_max(i, 2 * half)
                if 0 <= a < U:
                    do_scores_exp(a, half)
                    do_exp(a, half)
                advance()
                if i < U:
                    do_scores_max(i, 2 * half + 1)
                    do_max(i, 2 * half + 1)
                if v >= 0:
                    do_pv(v, half)
                if v >= 0 and v % H == H - 1:
                    do_norm_scale(v // H) if half == 0 else do_norm(v // H)
                if half == 0:
                    advance()
            if i < U and i % 2 == 1:
                do_bias(i - 1)
            if 0 <= a < U:
                do_turn(a)
                t_over = a // H
                if t_over > 0 and a % 4 in (1, 3) and a % H > LAG_X:
                    load_weights(t_over, (scored2[2 * t_over * H - 1], scored[4 * t_over * H - 1]))
            if v >= 0 and v % H == H - 1:
                to_close.append((v // H, close_layer(v // H)))
            advance()
        over = (maxd[4 * U - 1], expd[2 * U - 1], normd[NT - 1], turnd[U - 1], pvd[U - 1])
        sp.need(*over)
        while slots_asked[0] <= E:
            ask_weights(over)
        pe.need(*over)
        dve.need(*over)
        act.need(*over)
        room = words[:].rearrange("p b t -> p (b t)").bitcast(F32)
        R, NY = 4, 3
        gu = room[:, 0:R * 2 * P].rearrange("p (r f) -> p r f", r=R)
        th = room[:, R * 2 * P:R * 3 * P].rearrange("p (r f) -> p r f", r=R)
        hid = room[:, R * 3 * P:R * 4 * P].rearrange("p (r f) -> p r f", r=R)
        hidT = arena[:, (E + 1) * FE:(E + 1) * FE + R * P].rearrange("p (r f) -> p r f", r=R)
        y_sb = room[:, R * 4 * P:R * 4 * P + NY * D].rearrange("p (r f) -> p r f", r=NY)
        room2 = pT[:].rearrange("p b n t -> p (b n t)").bitcast(F32)
        NX, NXT = 4, 3
        xg = room2[:, 0:NX * D].rearrange("p (r f) -> p r f", r=NX)
        xgT = room2[:, NX * D:(NX + NXT) * D].rearrange("p (r c t) -> p r c t", r=NXT, c=C)
        moved = room2[:, (NX + NXT) * D:(NX + NXT) * D + NT * K * E].rearrange("p (n k e) -> p n k e", n=NT, k=K)
        half_gate = sb("half_gate", [P, 1])
        then(nc.vector.tensor_scalar(half_gate[:], gates[:, 1:2], 0.5, None, ALU.mult))
        EARLY = 6
        TILES = [("shared", t) for t in range(EARLY)] + [("expert", g) for g in range(NTILE)] + \
                [("shared", t) for t in range(EARLY, NT)]
        ld_xg = [stage(f"ld_xg{n}", 16) for n in range(NX)]
        st_y = [stage(f"st_y{n}", 16) for n in range(NY)]
        names = ("t_turn", "t_copy", "t_gu", "t_clip", "t_tanh", "t_gate", "t_hid", "t_hturn", "t_hcopy", "t_down", "t_out")
        st = {n: stage(n) for n in names}
        done = {n: {} for n in names}
        fetched, stored, expert_of = {}, {}, {}

        def mark(name, j, ins):
            done[name][j] = st[name].mark(ins)

        def fetch(j):
            if j < len(TILES) and TILES[j][0] == "expert":
                g = TILES[j][1]
                pool.need(done["t_turn"].get(j - NX), (st_xn.sem, st_xn.count), rows_step[0])
                fetched[j] = ld_xg[g % NX].mark(nc.gpsimd.indirect_dma_start(
                    out=xg[:, g % NX, :], out_offset=None, in_=io["x_norm"],
                    in_offset=bass.IndirectOffsetOnAxis(ap=rows_i[:, g:g + 1].bitcast(U32), axis=0)))

        def turn_rows(j):
            kind, g = TILES[j]
            if kind == "expert":
                pe.need(fetched[j], done["t_copy"].get(j - 2))
                for c in range(C):
                    ins = nc.tensor.transpose(bank(j % 2)[:, c * P:(c + 1) * P], xg[:, g % NX, c * P:(c + 1) * P], ident[:])
                mark("t_turn", j, ins)
                act.need(done["t_turn"][j], done["t_gu"].get(j - NXT))
                mark("t_copy", j, nc.scalar.copy(xgT[:, j % NXT].rearrange("p c t -> p (c t)"), bank(j % 2)[:, 0:D]))

        def name_expert(j):
            kind, g = TILES[j]
            if kind == "shared":
                pe.need(slots_got[0])
                expert_of[j] = 0
            else:
                pe.need(slots_got[E - 1], slots_got[E], expert_step[0])
                expert_of[j] = nc.tensor.value_load(expert_i[0:1, g:g + 1], min_val=1, max_val=E)

        def gate_up(j):
            kind, t = TILES[j]
            b = (0 if j < EARLY else 2) + j % 2
            pe.need(done["t_clip"].get(j - 2), done["t_copy"][j] if kind == "expert" else x2T_ready[t])
            src = xgT[:, j % NXT] if kind == "expert" else x2T[:, :, t * P:(t + 1) * P]
            for c in range(C):
                w = W[:, bass.ds(expert_of[j], 1), c * 2 * I:(c + 1) * 2 * I].rearrange("p o f -> p (o f)")
                ins = nc.tensor.matmul(bank(b)[:, 0:2 * I], src[:, c, :], w, start=(c == 0), stop=(c == C - 1))
            mark("t_gu", j, ins)
            dve.need(done["t_gu"][j], done["t_hid"].get(j - R), done["t_tanh"].get(j - R))
            mark("t_clip", j, nc.vector.tensor_scalar(gu[:, j % R, :], bank(b)[:, 0:2 * I], 7.0, -7.0, ALU.min, ALU.max))
            act.need(done["t_clip"][j], done["t_gate"].get(j - R))
            mark("t_tanh", j, nc.scalar.activation(th[:, j % R, :], gu[:, j % R, 0:I], ACT.Tanh, scale=0.5))

        def hidden(j):
            q = j % R
            dve.need(done["t_tanh"][j], done["t_hturn"].get(j - R))
            mark("t_gate", j, nc.vector.scalar_tensor_tensor(out=hid[:, q, :], in0=th[:, q, :], scalar=1.0,
                                                             in1=gu[:, q, 0:I], op0=ALU.add, op1=ALU.mult))
            dve.need(done["t_gate"][j])
            mark("t_hid", j, nc.vector.tensor_tensor(hid[:, q, :], hid[:, q, :], gu[:, q, I:2 * I], ALU.mult))

        def turn_hidden(j):
            pe.need(done["t_hid"][j], done["t_hcopy"].get(j - 2))
            mark("t_hturn", j, nc.tensor.transpose(bank(4 + j % 2)[:, 0:P], hid[:, j % R, :], ident[:]))
            dve.need(done["t_hturn"][j], done["t_down"].get(j - R))
            mark("t_hcopy", j, nc.vector.tensor_copy(hidT[:, j % R, :], bank(4 + j % 2)[:, 0:P]))

        def down(j):
            kind, t = TILES[j]
            o = bank(6 + j % 2)[:, 0:D]
            pe.need(done["t_hcopy"][j], done["t_out"].get(j - 2))
            w = W[:, bass.ds(expert_of.pop(j), 1), 2 * C * I:FE].rearrange("p o f -> p (o f)")
            mark("t_down", j, nc.tensor.matmul(o, hidT[:, j % R, :], w, start=True, stop=True))
            if kind == "shared":
                dve.need(done["t_down"][j])
                done["t_out"][j] = shared_in[t] = t_shared.mark(nc.vector.scalar_tensor_tensor(
                    out=x_sb[:, t, :], in0=o, scalar=half_gate[:], in1=x_sb[:, t, :], op0=ALU.mult, op1=ALU.add))
                return
            act.need(done["t_down"][j], stored.get(t - NY))
            mark("t_out", j, nc.scalar.copy(y_sb[:, t % NY, :], o))
            sp.need(done["t_out"][j])
            stored[t] = st_y[t % NY].mark(nc.sync.dma_start(io["y_rows"][t * P:(t + 1) * P, :], y_sb[:, t % NY, :]))

        shared_in = {}
        t_shared = stage("t_shared")
        LAGS = ((0, turn_rows), (5, turn_hidden), (2, gate_up), (1, name_expert), (3, hidden), (6, down))

        def run_tiles(first, last, beside=None):
            for i in range(first, last + 6):
                for lag, step in LAGS:
                    if first <= i - lag < last:
                        step(i - lag)
                        if lag == 0 and i + NX < last:
                            fetch(i + NX)
                if beside:
                    beside()

        rows_step, expert_step = [None], [None]

        def advance_some():
            for _ in range(12):
                advance()

        run_tiles(0, EARLY, advance_some)
        while to_close or to_route:
            advance()

        spare = v_corr[:].rearrange("p n d -> p (n d)").bitcast(F32)
        count = sb("count", [P, E])
        ntile = sb("ntile", [P, E])
        ends = [sb(f"ends{n}", [P, E]) for n in range(2)]
        le = sb("le", [P, E])
        tmp = sb("tmp", [P, E])
        tile_no = sb("tile_no", [P, 1])
        e_t = sb("e_t", [P, 1])
        first = sb("first", [P, 1])
        first_i = sb("first_i", [P, 1], I32)
        lists = spare[:, 0:P]
        s1 = sb("s1", [P, 2])
        spread = spare[:, P:2 * P]
        rows_i = spare[:, 3 * P:4 * P].bitcast(I32)
        expert_i = sb("expert_i", [1, P], I32)
        ones_f = spare[:, 2 * P:3 * P]
        pe.need(by_now("pool"), done["t_clip"][EARLY - 1])
        counted = does("pe", nc.tensor.matmul(bank(3)[:, 0:E], ones_sq[:], load[:], start=True, stop=True))
        dve.need(counted)
        then(nc.vector.memset(ones_f, 1.0))
        then(nc.vector.tensor_copy(count[:], bank(3)[:, 0:E]))
        then(nc.vector.tensor_scalar(tmp[:], count[:], float(P - 1), 1.0 / P, ALU.add, ALU.mult))
        then(nc.vector.tensor_scalar(tmp[:], tmp[:], 0.5 - 0.5 / P, ROUND, ALU.subtract, ALU.add))
        then(nc.vector.tensor_scalar(ntile[:], tmp[:], ROUND, None, ALU.subtract))
        then(nc.vector.tensor_copy(ends[0][:], ntile[:]))
        step, q = 1, 0
        while step < E:
            nc.vector.tensor_copy(ends[1 - q][:, 0:step], ends[q][:, 0:step])
            then(nc.vector.tensor_tensor(ends[1 - q][:, step:E], ends[q][:, step:E], ends[q][:, 0:E - step], ALU.add))
            step, q = 2 * step, 1 - q
        end = ends[q]
        then(nc.vector.tensor_scalar(s1[:, 0:1], end[:, E - 1:E], -1.0, None, ALU.add))
        then(nc.vector.tensor_scalar(tile_no[:], lane[:], s1[:, 0:1], None, ALU.min))
        then(nc.vector.tensor_scalar(le[:], end[:], tile_no[:], None, ALU.is_le))
        then(nc.vector.tensor_reduce(e_t[:], le[:], AX.X, ALU.add))
        then(nc.vector.tensor_tensor(tmp[:], le[:], end[:], ALU.mult))
        then(nc.vector.tensor_reduce(s1[:, 1:2], tmp[:], AX.X, ALU.max))
        then(nc.vector.tensor_scalar(first[:], tile_no[:], s1[:, 1:2], None, ALU.subtract))
        then(nc.vector.tensor_scalar(s1[:, 0:1], e_t[:], float(REGION // P), None, ALU.mult))
        then(nc.vector.tensor_scalar(first_i[:], first[:], s1[:, 0:1], None, ALU.add))
        first_ready = (chain.sem, chain.count)
        then(nc.vector.tensor_scalar(spread, ident[:], e_t[:], None, ALU.mult))
        ld_list = stage("ld_list", 16)
        pool.need((st_x.sem, st_x.count), first_ready)
        got_list = ld_list.mark(nc.gpsimd.indirect_dma_start(
            out=lists, out_offset=None, in_=io["slots"].rearrange("(r p) o -> r (p o)", p=P),
            in_offset=bass.IndirectOffsetOnAxis(ap=first_i[:, 0:1].bitcast(U32), axis=0)))
        pe.need((chain.sem, chain.count))
        a = does("pe", nc.tensor.matmul(bank(3)[:, 0:P], ones_f, spread, start=True, stop=True))
        dve.need(a)
        then(nc.vector.tensor_scalar(expert_i[:], bank(3)[0:1, 0:P], 1.0, None, ALU.add))
        expert_step[0] = (chain.sem, chain.count)
        pe.need(got_list, expert_step[0])
        a = does("pe", nc.tensor.transpose(bank(3)[:, 0:P], lists, ident[:]))
        dve.need(a)
        then(nc.vector.tensor_copy(rows_i, bank(3)[:, 0:P]))
        rows_step[0] = (chain.sem, chain.count)
        for j in range(EARLY, EARLY + NX):
            fetch(j)
        shift = sb("shift", [P, E])
        pick = xn[:, 0:NT // 2, :].rearrange("p n d -> p (n d)").rearrange("p (n k e) -> p n k e", n=NT, k=K)
        weight = xn[:, NT // 2:NT // 2 + 2, :].rearrange("p n d -> p (n d)").rearrange("p (n e) -> p n e", n=NT)
        total = sb("total", [P, NT])
        dve.need((st_xn.sem, st_xn.count))
        y_f = sb("y_f", [P, NT, K])
        y_i = sb("y_i", [P, NT * K], I32)
        over_k = [P, NT, K, E]
        top_k = top_keys[:, :, 0:K]
        y_step = [None]

        def places():
            then(nc.vector.tensor_tensor(shift[:], end[:], ntile[:], ALU.subtract))
            yield
            then(nc.vector.tensor_scalar(shift[:], shift[:], float(P), None, ALU.mult))
            yield
            then(nc.vector.tensor_tensor(shift[:], shift[:], region0[:], ALU.subtract))
            yield
            then(nc.vector.tensor_tensor(pick, keys[:].unsqueeze(2).broadcast_to(over_k),
                                         top_k.unsqueeze(3).broadcast_to(over_k), ALU.is_equal))
            yield
            then(nc.vector.tensor_tensor(moved.rearrange("p n k e -> p (n k) e"), pick.rearrange("p n k e -> p (n k) e"),
                                         shift[:].unsqueeze(1).broadcast_to([P, NT * K, E]), ALU.mult))
            yield
            then(nc.vector.tensor_reduce(y_f[:], moved, AX.X, ALU.add))
            yield
            then(nc.vector.tensor_tensor(y_f[:], y_f[:], top_k, ALU.subtract))
            yield
            then(nc.vector.tensor_scalar(y_i[:], y_f[:].rearrange("p n k -> p (n k)"), BIG, None, ALU.add))
            y_step[0] = (chain.sem, chain.count)
            yield
            yield
            then(nc.vector.tensor_scalar(weight, keys[:], 0.0, None, ALU.is_gt))
            yield
            then(nc.vector.tensor_tensor(weight, weight, score_e[:], ALU.mult))
            yield
            then(nc.vector.tensor_reduce(total[:], weight, AX.X, ALU.add))
            yield
            then(nc.vector.tensor_scalar(total[:], total[:], 1e-20, None, ALU.add))
            yield
            then(nc.vector.reciprocal(total[:], total[:]))
            yield
            then(nc.vector.tensor_scalar(total[:], total[:], 0.5, gates[:, 1:2], ALU.mult, ALU.mult))
            yield
            then(nc.vector.tensor_tensor(weight, weight, total[:].unsqueeze(2).broadcast_to([P, NT, E]), ALU.mult))
            yield
            then(nc.vector.tensor_tensor(moved, pick, weight.unsqueeze(2).broadcast_to(over_k), ALU.mult))
            yield
            then(nc.vector.tensor_reduce(share[:], moved, AX.X, ALU.add))

        NG = 8
        yg = moved.rearrange("p n k e -> p (n k e)").rearrange("p (g d) -> p g d", g=NG)
        ld_yg = [stage(f"ld_yg{n}", 16) for n in range(NG)]
        s_acc = stage("s_acc")
        st_o = stage("st_o", 16)

        def gather():
            acc = []
            pool.need(y_step[0], place_step[0], *(stored[g] for g in range(NTILE - NY, NTILE)))
            for m in range(NT * K):
                t, k = divmod(m, K)
                while t not in shared_in:
                    yield
                pool.need(acc[m - NG] if m >= NG else None)
                got = ld_yg[m % NG].mark(nc.gpsimd.indirect_dma_start(
                    out=yg[:, m % NG, :], out_offset=None, in_=io["y_rows"],
                    in_offset=bass.IndirectOffsetOnAxis(ap=y_i[:, m:m + 1].bitcast(U32), axis=0)))
                if m >= BEHIND:
                    add_row(m - BEHIND, acc, gots)
                gots[m] = got
                yield
            for m in range(NT * K - BEHIND, NT * K):
                add_row(m, acc, gots)

        BEHIND = 3
        gots = {}

        def add_row(m, acc, gots):
            t, k = divmod(m, K)
            dve.need(gots.pop(m), acc[-1] if acc else None, shared_in[t])
            acc.append(s_acc.mark(nc.vector.scalar_tensor_tensor(out=x_sb[:, t, :], in0=yg[:, m % NG, :],
                                                                 scalar=share[:, t, k:k + 1], in1=x_sb[:, t, :],
                                                                 op0=ALU.mult, op1=ALU.add)))
            if k == K - 1:
                sp.need(acc[-1])
                st_o.mark(nc.sync.dma_start(io["out"].rearrange("(n p) d -> n p d", p=P)[t], x_sb[:, t, :]))

        place_step = [None]
        place, gathering = places(), gather()

        def beside():
            if next(place, "over") == "over" and place_step[0] is None:
                place_step[0] = (chain.sem, chain.count)
            if len(stored) == NTILE:
                next(gathering, None)
                next(gathering, None)

        run_tiles(EARLY, len(TILES), beside)
        for _ in gathering:
            pass
        sp.need((st_o.sem, st_o.count))
        close_scope()


def kernel(x, ctx_2048, g_xattn, g_ffn, L0_xattn_Wq, L0_xattn_bq, L0_xattn_Wkv, L0_xattn_bkv, L0_xattn_Wp,
           L0_xattn_bp, L0_ffn_router_w, L0_ffn_expert_bias, L0_ffn_gate_w, L0_ffn_up_w, L0_ffn_down_w,
           L0_ffn_shared_gate_w, L0_ffn_shared_up_w, L0_ffn_shared_down_w):
    import concourse.bacc as bacc
    from concourse.bass_utils import run_bass_kernel_spmd as run

    n = np.asarray
    D = x.shape[-1]
    bkv = n(L0_xattn_bkv)
    gate = np.concatenate([n(L0_ffn_shared_gate_w)[None], n(L0_ffn_gate_w)])
    up = np.concatenate([n(L0_ffn_shared_up_w)[None], n(L0_ffn_up_w)])
    down = np.concatenate([n(L0_ffn_shared_down_w)[None], n(L0_ffn_down_w)])
    parts = []
    for c in range(D // 128):
        parts += [gate[:, :, c * 128:(c + 1) * 128].transpose(2, 0, 1), up[:, :, c * 128:(c + 1) * 128].transpose(2, 0, 1)]
    experts = np.concatenate(parts + [down.transpose(2, 0, 1)], axis=2).reshape(128, -1)
    arrays = {
        "x": n(x).reshape(-1, D),
        "ctxT": n(ctx_2048).reshape(-1, D).T,
        "wq": n(L0_xattn_Wq), "wkv": n(L0_xattn_Wkv), "wp": n(L0_xattn_Wp),
        "rows": np.concatenate([n(L0_xattn_bq), bkv[:D], n(L0_xattn_bp), n(g_xattn).reshape(1),
                                n(g_ffn).reshape(1)])[None, :],
        "bv": bkv[D:].reshape(-1, 128).T,
        "router_wT": n(L0_ffn_router_w).T,
        "expert_bias": n(L0_ffn_expert_bias)[None, :],
        "experts": experts,
    }
    arrays = {k: np.ascontiguousarray(a) for k, a in arrays.items()}
    nc = bacc.Bacc("TRN2", target_bir_lowering=False, num_devices=1)
    io = {k: nc.dram_tensor(f"in_{k}", a.shape, mybir.dt.from_np(a.dtype), kind="ExternalInput").ap()
          for k, a in arrays.items()}
    T = arrays["x"].shape[0]
    io["out"] = nc.dram_tensor("out_y", (T, D), F32, kind="ExternalOutput").ap()
    E, K = arrays["router_wT"].shape[1], 4
    io["slots"] = nc.dram_tensor("slots", (E * (T + 128), 1), F32, kind="Internal").ap()
    io["x_norm"] = nc.dram_tensor("x_norm", (T, D), F32, kind="Internal").ap()
    io["y_rows"] = nc.dram_tensor("y_rows", (((T * K - E) // 128 + E) * 128, D), F32, kind="Internal").ap()
    build(nc, io)
    r = run(nc, [{f"in_{k}": a for k, a in arrays.items()}], core_ids=[0])
    return r.results[0]["out_y"].reshape(x.shape)
```
